# Optimizing a Trainium2 kernel written in Bass

```python
import numpy as np
import jax
import jax.numpy as jnp

def _softmax(x, axis=-1):
    return jax.nn.softmax(x, axis=axis)

def _gelu(x):
    return jax.nn.gelu(x, approximate=True)

def _silu(x):
    return jax.nn.silu(x)

def _sigmoid(x):
    return jax.nn.sigmoid(x)

def _layernorm(x, axis=-1, eps=1e-05):
    m = jnp.mean(x, axis=axis, keepdims=True)
    v = jnp.var(x, axis=axis, keepdims=True)
    return (x - m) / jnp.sqrt(v + eps)

def _scatter_add(tgt, idx, src, axis=0):
    return tgt.at[idx].add(src)

def _segment_sum(src, seg, n):
    return jax.ops.segment_sum(src, seg, n)
kernel_name = 'mk_adaln_d1_jaxref_r8_ac5a52'

def setup_inputs(seed: int=0):
    np.random.seed(seed)
    _w = jnp.asarray

    def _L0_attn_setup():
        import jax, jax.numpy as jnp
        import numpy as np
        import math
        DIM = 128
        H = 16
        D = 64
        M = 64
        B = 1
        N = 256

        def _orf_omega(key):
            blocks = []
            n_blocks = (M + D - 1) // D
            for i in range(n_blocks):
                G = jax.random.normal(jax.random.fold_in(key, i), (D, D), dtype=jnp.float32)
                Q, _ = jnp.linalg.qr(G)
                blocks.append(Q.T)
            return jnp.concatenate(blocks, axis=0)[:M]

        def _phi(x, omega):
            proj = jnp.einsum('bhnd,md->bhnm', x, omega)
            norm = 0.5 * jnp.sum(x * x, axis=-1, keepdims=True)
            return jnp.exp(proj - norm) / math.sqrt(M)

        def _heads(t):
            b, n, _ = t.shape
            return t.reshape(b, n, H, D).transpose(0, 2, 1, 3)
        key = jax.random.key(seed)
        ks = jax.random.split(key, 7)
        inner = H * D
        x = jax.random.normal(ks[0], (B, N, DIM), dtype=jnp.float32)
        omega = _orf_omega(ks[1])
        wq = jax.random.normal(ks[2], (inner, DIM), dtype=jnp.float32) * 0.02
        wk = jax.random.normal(ks[3], (inner, DIM), dtype=jnp.float32) * 0.02
        wv = jax.random.normal(ks[4], (inner, DIM), dtype=jnp.float32) * 0.02
        wo = jax.random.normal(ks[5], (DIM, inner), dtype=jnp.float32) * 0.02
        bo = jnp.zeros((DIM,), dtype=jnp.float32)
        return {'x': x, 'omega': omega, 'wq': wq, 'wk': wk, 'wv': wv, 'wo': wo, 'bo': bo}
    _L0_attn_in = _L0_attn_setup()

    def _L0_ffn_setup():
        import math
        import jax, jax.numpy as jnp
        import numpy as np
        K = 2
        CAP_FACTOR = 1.0
        EPS = 1e-09
        key = jax.random.key(seed)
        ks = jax.random.split(key, 6)
        B, S, D, H, E = (4, 256, 128, 512, 8)
        x = jax.random.normal(ks[0], (B, S, D), jnp.float32)
        wg = jax.random.normal(ks[1], (D, E), jnp.float32) * 0.02
        w1 = jax.random.normal(ks[2], (E, D, H), jnp.float32) * 0.02
        b1 = jnp.zeros((E, H), jnp.float32)
        w2 = jax.random.normal(ks[3], (E, H, D), jnp.float32) * 0.02
        b2 = jnp.zeros((E, D), jnp.float32)
        return {'x': x, 'wg': wg, 'w1': w1, 'b1': b1, 'w2': w2, 'b2': b2}
    _L0_ffn_in = _L0_ffn_setup()
    _L0_c = _w((lambda *s: np.random.randn(*s).astype(np.float32) * 0.05)(4, 128))
    _L0_wmod = _w((lambda *s: np.random.randn(*s).astype(np.float32) * 0.05)(128, 6 * 128) * 128 ** (-0.5))
    _d = {'L0_attn_x': _L0_attn_in['x'], 'L0_attn_omega': _L0_attn_in['omega'], 'L0_attn_wq': _L0_attn_in['wq'], 'L0_attn_wk': _L0_attn_in['wk'], 'L0_attn_wv': _L0_attn_in['wv'], 'L0_attn_wo': _L0_attn_in['wo'], 'L0_attn_bo': _L0_attn_in['bo'], 'L0_ffn_wg': _L0_ffn_in['wg'], 'L0_ffn_w1': _L0_ffn_in['w1'], 'L0_ffn_b1': _L0_ffn_in['b1'], 'L0_ffn_w2': _L0_ffn_in['w2'], 'L0_ffn_b2': _L0_ffn_in['b2'], 'L0_c': _L0_c, 'L0_wmod': _L0_wmod}
    _x0 = _d['L0_attn_x']
    _d['L0_attn_x'] = jax.random.normal(jax.random.fold_in(jax.random.key(seed), 1), (4, 1024, 128), dtype=_x0.dtype)
    del _x0
    return _d

def reference(L0_attn_x, L0_attn_omega, L0_attn_wq, L0_attn_wk, L0_attn_wv, L0_attn_wo, L0_attn_bo, L0_ffn_wg, L0_ffn_w1, L0_ffn_b1, L0_ffn_w2, L0_ffn_b2, L0_c, L0_wmod):

    def _L0_attn_ref(x, omega, wq, wk, wv, wo, bo):
        import jax, jax.numpy as jnp
        import numpy as np
        import math
        DIM = 128
        H = 16
        D = 64
        M = 64
        B = 1
        N = 256

        def _orf_omega(key):
            blocks = []
            n_blocks = (M + D - 1) // D
            for i in range(n_blocks):
                G = jax.random.normal(jax.random.fold_in(key, i), (D, D), dtype=jnp.float32)
                Q, _ = jnp.linalg.qr(G)
                blocks.append(Q.T)
            return jnp.concatenate(blocks, axis=0)[:M]

        def _phi(x, omega):
            proj = jnp.einsum('bhnd,md->bhnm', x, omega)
            norm = 0.5 * jnp.sum(x * x, axis=-1, keepdims=True)
            return jnp.exp(proj - norm) / math.sqrt(M)

        def _heads(t):
            b, n, _ = t.shape
            return t.reshape(b, n, H, D).transpose(0, 2, 1, 3)
        b, n, _ = x.shape
        q = _heads(x @ wq.T)
        k = _heads(x @ wk.T)
        v = _heads(x @ wv.T)
        phi_q = _phi(q, omega)
        phi_k = _phi(k, omega)
        kv = jnp.einsum('bhnm,bhnd->bhnmd', phi_k, v)
        kv_cumsum = jnp.cumsum(kv, axis=2)
        k_cumsum = jnp.cumsum(phi_k, axis=2)
        out = jnp.einsum('bhnm,bhnmd->bhnd', phi_q, kv_cumsum)
        z = 1.0 / (jnp.einsum('bhnm,bhnm->bhn', phi_q, k_cumsum) + 1e-06)
        out = out * z[..., None]
        out = out.transpose(0, 2, 1, 3).reshape(b, n, H * D)
        return out @ wo.T + bo

    def _L0_ffn_ref(x, wg, w1, b1, w2, b2):
        import math
        import jax, jax.numpy as jnp
        import numpy as np
        K = 2
        CAP_FACTOR = 1.0
        EPS = 1e-09
        B, S, D = x.shape
        E = wg.shape[1]
        xt = x.reshape(-1, D)
        N = xt.shape[0]
        cap = int(math.ceil(CAP_FACTOR * K * N / E))
        logits = xt.astype(jnp.float32) @ wg.astype(jnp.float32)
        scores = jax.nn.softmax(logits, axis=-1)
        gvals, gidx = jax.lax.top_k(scores, K)
        gvals = gvals / jnp.clip(gvals.sum(-1, keepdims=True), EPS)
        offset = jnp.zeros((E,), jnp.int32)
        pos_l, keep_l = ([], [])
        for kk in range(K):
            m = jax.nn.one_hot(gidx[:, kk], E, dtype=jnp.int32)
            loc = jnp.cumsum(m, axis=0) - 1 + offset[None, :]
            offset = offset + m.sum(axis=0)
            pos = jnp.take_along_axis(loc, gidx[:, kk:kk + 1], axis=1)[:, 0]
            keep = pos < cap
            pos_l.append(jnp.where(keep, pos, 0))
            keep_l.append(keep)
        pos = jnp.stack(pos_l, axis=1)
        keep = jnp.stack(keep_l, axis=1)
        gvals = gvals * keep
        e_flat = gidx.reshape(-1)
        p_flat = pos.reshape(-1)
        kmask = keep.reshape(-1).astype(x.dtype)
        x_rep = jnp.repeat(xt, K, axis=0)
        disp = jnp.zeros((E, cap, D), x.dtype).at[e_flat, p_flat].add(x_rep * kmask[:, None])
        h = jax.nn.gelu(jnp.einsum('ecd,edh->ech', disp, w1) + b1[:, None, :], approximate=False)
        y = jnp.einsum('ech,ehd->ecd', h, w2) + b2[:, None, :]
        yk = y[e_flat, p_flat]
        w = gvals.reshape(-1).astype(x.dtype)
        out = (yk * w[:, None]).reshape(N, K, D).sum(axis=1)
        return out.reshape(B, S, D)
    x = L0_attn_x
    mod = (_silu(L0_c) @ L0_wmod).reshape(L0_c.shape[0], 6, 1, -1)
    sa, ca, ga, sb, cb, gb = (mod[:, 0], mod[:, 1], mod[:, 2], mod[:, 3], mod[:, 4], mod[:, 5])
    ga = (2 * (ga >= 0) - 1) * jnp.maximum(jnp.abs(ga), 0.25)
    gb = (2 * (gb >= 0) - 1) * jnp.maximum(jnp.abs(gb), 0.25)
    h = _layernorm(x, axis=-1) * (1 + ca) + sa
    x = x + ga * _L0_attn_ref(h, L0_attn_omega, L0_attn_wq, L0_attn_wk, L0_attn_wv, L0_attn_wo, L0_attn_bo)
    h = _layernorm(x, axis=-1) * (1 + cb) + sb
    x = x + gb * _L0_ffn_ref(h, L0_ffn_wg, L0_ffn_w1, L0_ffn_b1, L0_ffn_w2, L0_ffn_b2)
    return x

_drawn_inputs = setup_inputs


def setup_inputs(seed=0):
    import zlib

    import numpy as np

    out = dict(_drawn_inputs(seed))
    spreads = {'L0_attn_bo': (0.0, 0.32), 'L0_ffn_b1': (0.0, 0.8), 'L0_ffn_b2': (0.0, 0.465)}
    factors = {'L0_attn_omega': 8.0,
     'L0_attn_wq': 8.0,
     'L0_attn_wk': 8.0,
     'L0_attn_wv': 8.0,
     'L0_attn_wo': 8.0,
     'L0_ffn_wg': 3.209,
     'L0_ffn_w1': 6.043,
     'L0_ffn_w2': 5.489}
    for name, (base, spread) in spreads.items():
        noise = np.random.default_rng([zlib.crc32(name.encode()), seed]).standard_normal(out[name].shape)
        drawn = base * np.exp(spread * noise) if base else spread * noise
        out[name] = jnp.asarray(drawn.astype(out[name].dtype))
    for name, factor in factors.items():
        out[name] = (out[name] * factor).astype(out[name].dtype)
    return out
```

```python
from contextlib import ExitStack

import concourse.bass as bass
from concourse import mybir

F32 = mybir.dt.float32
F32R = mybir.dt.float32r
BF16 = mybir.dt.bfloat16
I32 = mybir.dt.int32
U32 = mybir.dt.uint32
ALU = mybir.AluOpType
ACT = mybir.ActivationFunctionType
AX = mybir.AxisListType.X

P = 128


def build(nc, x, omega, wq, wk, wv, wo, bo, wg, w1, b1, w2, b2, cond, wmod, out):
    B, S, D = x.shape
    M, DH = omega.shape
    HD = wq.shape[0]
    H = HD // DH
    NP = H // 2
    E, _, HID = w1.shape
    KH = HID // P
    N = B * S
    NCH = N // P
    CPB = S // P
    SHIFT = CPB.bit_length() - 1
    CAP = (2 * N + E - 1) // E
    NSL = E * CAP // P
    TPE = CAP // P
    GS = 4
    NG = NSL // GS
    KC = 2 * NCH
    VW = DH + 1
    PW = 2 * VW
    SKIP = 200000
    FEATURE_SCALE = float(M) ** -0.5
    assert D == P and DH == 64 and M == 64 and CAP % (GS * P) == 0 and HD == 1024

    h2_rows = nc.dram_tensor("h2_rows", [N, D], F32, kind="Internal").ap()
    y_rows = nc.dram_tensor("y_rows", [2 * N, D], F32, kind="Internal").ap()

    with ExitStack() as ctx:
        def sb(name, shape, dt=F32):
            return ctx.enter_context(nc.sbuf_tensor(name, shape, dt))

        sems = {}

        def sem(name):
            if name not in sems:
                sems[name] = ctx.enter_context(nc.semaphore(name))
            return sems[name]

        def times(count, most=None):
            if not isinstance(count, int):
                return count
            return max(count, 0) if most is None else min(max(count, 0), most)

        def apart(eng):
            eng.sem_inc(sem("wait_passed"), 1)

        x_sb = sb("x_sb", [P, NCH * D])
        wT_hi = {k: sb(f"w{k}_hi", [P, HD], F32R) for k in ("q", "k", "v", "pq", "pk")}
        wT_lo = {k: sb(f"w{k}_lo", [P, HD], F32R) for k in ("q", "k", "v", "pq", "pk")}
        woT = sb("woT", [P, NP, D])
        wg_sb = sb("wg_sb", [P, E])
        ident = sb("ident", [P, P])
        causal = sb("causal", [P, 4, P])
        keep = sb("keep", [P, NCH], U32)
        sa_col = sb("sa_col", [P, B + 1])
        ca_col = sb("ca_col", [P, B + 1])
        ga_b = sb("ga_b", [P, (B + 1) * D])
        sb_b = sb("sb_b", [P, (B + 1) * D])
        cb_b = sb("cb_b", [P, (B + 1) * D])
        gb_b = sb("gb_b", [P, (B + 1) * D])
        bo_b = sb("bo_b", [P, D])
        b2_b = sb("b2_b", [P, E * D])
        b1_col = sb("b1_col", [P, E * KH])
        logits = sb("logits", [P, NCH * E])

        psum = [ctx.enter_context(nc.psum_tensor(f"bank{i}", [P, 512], F32)) for i in range(8)]

        x_v = x.rearrange("b (c p) d -> p (b c) d", p=P)
        out_v = out.rearrange("b (c p) d -> p (b c) d", p=P)

        def setup():
            with ExitStack() as tmp:
                def tsb(name, shape, dt=F32):
                    return tmp.enter_context(nc.sbuf_tensor(name, shape, dt))
                w_nat = {k: tsb(f"w{k}_nat", [P, NP, D]) for k in ("q", "k", "v")}
                wo_nat = tsb("wo_nat", [P, HD])
                om_blk = tsb("om_blk", [P, P])
                omT_blk = tsb("omT_blk", [P, P])
                c_nat = tsb("c_nat", [B, D])
                c_sig = tsb("c_sig", [B, D])
                c_silu = tsb("c_silu", [B, D])
                siluT = tsb("siluT", [P, B])
                silu_b = tsb("silu_b", [P, B, P])
                wmod_sb = tsb("wmod_sb", [P, 6 * D])
                b1_nat = tsb("b1_nat", [E * KH, P])
                sgn = tsb("sgn", [P, B * D])
                mag = tsb("mag", [P, B * D])
                zero = tsb("zero", [P, 2048])
                with nc.Block() as block:
                    @block.sync
                    def _(sp):
                        sp.dma_start(wo_nat[:], wo).then_inc(sem("s_wo"), 16)
                        for k, w in (("q", wq), ("k", wk), ("v", wv)):
                            sp.dma_start(w_nat[k][:], w.rearrange("(j p) d -> p j d", p=P)).then_inc(sem("qkv_loaded"), 16)
                        sp.dma_start(b1_nat[:], b1.rearrange("e (k p) -> (e k) p", p=P)).then_inc(sem("s_b1"), 16)
                        sp.wait_ge(sem("om_zeroed"), 1)
                        for i in range(2):
                            sp.dma_start(om_blk[i * M:(i + 1) * M, i * DH:(i + 1) * DH], omega).then_inc(sem("s_om"), 16)
                        for i in range(4):
                            n = NCH // 4
                            sp.dma_start(x_sb[:, i * n * D:(i + 1) * n * D].rearrange("p (c d) -> p c d", d=D),
                                         x_v[:, i * n:(i + 1) * n, :]).then_inc(sem("later_loads"), 16)
                        sp.wait_ge(sem("zeroed"), 1)
                        for i in range(4):
                            sp.dma_start(y_rows[i * 2048:(i + 1) * 2048, :].rearrange("(p r) d -> p (r d)", p=P),
                                         zero[:]).then_inc(sem("s_zero"), 16)
                        sp.wait_ge(sem("s_zero"), 64)

                    @block.scalar
                    def _(act):
                        act.dma_start(c_nat[:], cond).then_inc(sem("s_c"), 16)
                        act.dma_start(wmod_sb[:], wmod).then_inc(sem("s_wmod"), 16)
                        act.dma_start(wg_sb[:], wg).then_inc(sem("later_loads"), 16)
                        act.dma_start(bo_b[:], bo.rearrange("(a d) -> a d", a=1).to_broadcast([P, D])).then_inc(sem("later_loads"), 16)
                        act.dma_start(b2_b[:], b2.rearrange("(a e) d -> a (e d)", a=1).to_broadcast([P, E * D])).then_inc(sem("later_loads"), 16)
                        act.wait_ge(sem("s_c"), 16)
                        nc.scalar.activation(c_sig[:], c_nat[:], ACT.Exp, scale=-1.0).then_inc(sem("c_exp"), 1)
                        for n, (k, half) in enumerate(WEIGHTS):
                            act.wait_ge(sem("wT_filled"), n + 1)
                            nc.scalar.copy(wT_hi[k][:, half * 512:(half + 1) * 512], psum[n % 4][:]).then_inc(sem("wT_hi_done"), 1)

                    @block.gpsimd
                    def _(pool):
                        nc.gpsimd.memset(om_blk[:], 0.0).then_inc(sem("om_zeroed"), 1)
                        nc.gpsimd.memset(ident[:], 0.0).then_inc(sem("p_chain"), 1)
                        nc.gpsimd.memset(causal[:], 1.0).then_inc(sem("p_chain"), 1)
                        pool.wait_ge(sem("p_chain"), 2)
                        nc.gpsimd.affine_select(out=ident[:], in_=ident[:], compare_op=ALU.not_equal, fill=1.0, base=0,
                                                pattern=[[-1, P]], channel_multiplier=1).then_inc(sem("ident_ready"), 1)
                        nc.gpsimd.affine_select(out=causal[:], in_=causal[:], compare_op=ALU.is_ge, fill=0.0, base=0,
                                                pattern=[[0, 4], [1, P]], channel_multiplier=-1).then_inc(sem("p_chain"), 1)
                        nc.gpsimd.memset(zero[:], 0.0).then_inc(sem("zeroed"), 1)
                        pool.wait_ge(sem("p_chain"), 3)

                    @block.tensor
                    def _(pe):
                        pe.wait_ge(sem("ident_ready"), 1)
                        pe.wait_ge(sem("s_om"), 32)
                        pe.transpose(psum[7][:, 0:P], om_blk[:], ident[:]).then_inc(sem("small_filled"), 1)
                        pe.wait_ge(sem("silu_ready"), 1)
                        pe.wait_ge(sem("small_used"), 1)
                        pe.transpose(psum[7][:, 0:B], c_silu[:], ident[0:B, 0:B]).then_inc(sem("small_filled"), 1)
                        pe.wait_ge(sem("small_used"), 2)
                        pe.wait_ge(sem("s_b1"), 16)
                        pe.transpose(psum[7][:, 0:E * KH], b1_nat[:], ident[0:E * KH, 0:E * KH]).then_inc(sem("small_filled"), 1)
                        for n, (k, half) in enumerate(WEIGHTS):
                            if n >= 4:
                                pe.wait_ge(sem("wT_split"), times(n - 3))
                            dst = psum[n % 4]
                            src = w_nat[k[-1]]
                            pe.wait_ge(sem("qkv_loaded"), 48)
                            for j in range(4):
                                t = half * 4 + j
                                o = dst[:, j * P:(j + 1) * P]
                                if k in "qkv":
                                    mm = pe.transpose(o, src[:, t, :], ident[:])
                                else:
                                    mm = pe.matmul(o, src[:, t, :], omT_blk[:], start=True, stop=True)
                            mm.then_inc(sem("wT_filled"), 1)
                        pe.wait_ge(sem("s_wo"), 16)
                        for half in range(2):
                            for j in range(4):
                                t = half * 4 + j
                                mm = pe.transpose(psum[4 + half][:, j * P:(j + 1) * P], wo_nat[:, t * P:(t + 1) * P], ident[:])
                            mm.then_inc(sem("woT_filled"), 1)
                        pe.wait_ge(sem("s_wmod"), 16)
                        pe.wait_ge(sem("small_used"), 3)
                        pe.matmul(psum[7][:, 0:B], wmod_sb[:, 0:D], siluT[:], start=True, stop=True)
                        pe.matmul(psum[7][:, 64:64 + B], wmod_sb[:, D:2 * D], siluT[:], start=True, stop=True).then_inc(sem("mod_filled"), 1)
                        for m in range(4):
                            pe.wait_ge(sem("mod_used"), m)
                            for b in range(B):
                                mm = pe.matmul(psum[6][:, b * D:(b + 1) * D], silu_b[:, b, :],
                                               wmod_sb[:, (2 + m) * D:(3 + m) * D], start=True, stop=True)
                            mm.then_inc(sem("mod_filled"), 1)

                    @block.vector
                    def _(dve):
                        dve_n = [0]

                        def link(ins):
                            dve_n[0] += 1
                            ins.then_inc(sem("d_chain"), 1)
                            dve.wait_ge(sem("d_chain"), dve_n[0])
                        link(dve.memset(keep[:], 0xFFFFFFFF))
                        link(dve.memset(keep[:].rearrange("p (b c) -> p b c", c=CPB)[:, :, 0:1], 0))
                        dve.wait_ge(sem("small_filled"), 1)
                        dve.tensor_copy(omT_blk[:], psum[7][:, 0:P]).then_inc(sem("small_used"), 1)
                        dve.wait_ge(sem("c_exp"), 1)
                        link(dve.tensor_scalar(c_sig[:], c_sig[:], 1.0, None, ALU.add))
                        link(dve.reciprocal(c_sig[:], c_sig[:]))
                        dve.tensor_tensor(c_silu[:], c_nat[:], c_sig[:], ALU.mult).then_inc(sem("silu_ready"), 1)
                        dve.wait_ge(sem("small_filled"), 2)
                        link(dve.tensor_copy(siluT[:], psum[7][:, 0:B]))
                        dve.tensor_copy(silu_b[:], siluT[:].unsqueeze(2).to_broadcast([P, B, P])).then_inc(sem("small_used"), 1)
                        dve.wait_ge(sem("small_filled"), 3)
                        dve.tensor_copy(b1_col[:], psum[7][:, 0:E * KH]).then_inc(sem("small_used"), 1)
                        for n, (k, half) in enumerate(WEIGHTS):
                            dve.wait_ge(sem("wT_hi_done"), n + 1)
                            cols = slice(half * 512, (half + 1) * 512)
                            dve.tensor_tensor(wT_lo[k][:, cols], psum[n % 4][:], wT_hi[k][:, cols].bitcast(F32),
                                              ALU.subtract).then_inc(sem("wT_split"), 1)
                        for half in range(2):
                            dve.wait_ge(sem("woT_filled"), half + 1)
                            link(dve.tensor_copy(woT[:, half * 4:half * 4 + 4, :].rearrange("p j d -> p (j d)"), psum[4 + half][:]))
                        dve.wait_ge(sem("mod_filled"), 1)
                        link(dve.tensor_copy(sa_col[:, 0:B], psum[7][:, 0:B]))
                        link(dve.tensor_scalar(ca_col[:, 0:B], psum[7][:, 64:64 + B], 1.0, None, ALU.add))
                        for m, t in enumerate((ga_b, sb_b, cb_b, gb_b)):
                            dve.wait_ge(sem("mod_filled"), m + 2)
                            if t is sb_b:
                                dve.tensor_copy(t[:, 0:B * D], psum[6][:]).then_inc(sem("mod_used"), 1)
                            elif t is cb_b:
                                dve.tensor_scalar(t[:, 0:B * D], psum[6][:], 1.0, None, ALU.add).then_inc(sem("mod_used"), 1)
                            else:
                                link(dve.tensor_scalar(sgn[:], psum[6][:], 0.0, 2.0, ALU.is_ge, ALU.mult))
                                link(dve.tensor_scalar(mag[:], psum[6][:], -1.0, None, ALU.mult))
                                link(dve.tensor_tensor(mag[:], psum[6][:], mag[:], ALU.max))
                                link(dve.tensor_scalar(mag[:], mag[:], 0.25, None, ALU.max))
                                dve.scalar_tensor_tensor(out=t[:, 0:B * D], in0=sgn[:], scalar=-1.0, in1=mag[:],
                                                         op0=ALU.add, op1=ALU.mult).then_inc(sem("mod_used"), 1)
                        dve.wait_ge(sem("mod_used"), 4)
                        dve.wait_ge(sem("wT_split"), len(WEIGHTS))
                        dve.wait_ge(sem("later_loads"), 16 * 7)

        WEIGHTS = [(k, half) for k in ("q", "k", "v", "pq", "pk") for half in range(2)]
        setup()

        def attention():
            with ExitStack() as tmp:
                def tsb(name, shape, dt=F32):
                    return tmp.enter_context(nc.sbuf_tensor(name, shape, dt))
                xn = [tsb(f"xn{i}", [P, D]) for i in range(2)]
                st1 = tsb("st1", [P, 6])
                mv1 = tsb("mv1", [P, 2])
                rs1 = tsb("rs1", [P, 1])
                var1 = tsb("var1", [P, 1])
                var2 = tsb("var2", [P, 1])
                power = tsb("power", [P, 1])
                h_full = tsb("h_full", [P, P])
                h_hi = [tsb(f"h_hi{i}", [P, P], F32R) for i in range(2)]
                h_lo = [tsb(f"h_lo{i}", [P, P], F32R) for i in range(2)]
                square = {k: tsb(f"square_{k}", [P, HD]) for k in "qk"}
                norm = {k: tsb(f"norm_{k}", [P, H]) for k in "qk"}
                expo = {k: tsb(f"expo_{k}", [P, HD]) for k in "qk"}
                phi = {k: [tsb(f"phi_{k}{i}", [P, HD]) for i in range(2)] for k in "qk"}
                phiT = {k: tsb(f"phiT_{k}", [P, NP, P]) for k in "qk"}
                v_sb = [tsb(f"v_sb{i}", [P, H, VW]) for i in range(2)]
                scores = tsb("scores", [P, H, P])
                state = [tsb(f"state{i}", [P, NP, PW]) for i in range(2)]
                den = [tsb(f"den{i}", [P, 4]) for i in range(2)]
                rden = [tsb(f"rden{i}", [P, 4]) for i in range(2)]
                att = tsb("att", [P, H, DH])
                attT = tsb("attT", [P, NP, P])
                upd = [tsb(f"upd{i}", [P, D]) for i in range(2)]
                st2 = tsb("st2", [P, 6])
                mv2 = tsb("mv2", [P, 2])
                rs2 = tsb("rs2", [P, 1])
                xn2 = tsb("xn2", [P, D])
                xm2 = tsb("xm2", [P, D])
                h2T = tsb("h2T", [P, P])

                TURNS = {0: ["q0", "k0", "pq0", "pk0", "v0"], 1: ["q1", "k1", "pq1", "pk1", "v1"],
                         2: ["tk0", "tk1", "a0", "a2"], 3: ["tq0", "tq1", "a1", "a3"],
                         4: ["attT0", "o0", "o2"], 5: ["attT1", "o1", "o3"],
                         6: ["kv0", "kv1", "kv2"], 7: ["h2T", "lg", "wo", "hT"]}
                BANK = {k: b for b, ks in TURNS.items() for k in ks}
                BEFORE = {k: ks[i - 1] for ks in TURNS.values() for i, k in enumerate(ks)}

                def on_steps(eng, step):
                    for c in range(-2, 2):
                        step(c, c % 2)
                    with eng.Fori(1, NCH // 2 - 2) as i:
                        for j in range(2):
                            step(2 * i + j, j)
                    for c in range(NCH - 4, NCH + 2):
                        step(c, c % 2)

                def live(c, ahead=0):
                    return not isinstance(c, int) or 0 <= c + ahead < NCH

                with nc.Block() as block:
                    @block.tensor
                    def _(pe):
                        def project(kind, c, par):
                            if kind[:-1] == "q":
                                pe.wait_ge(sem(f"v{kind[-1]}_out"), times(c + 1))
                            else:
                                pe.wait_ge(sem(BEFORE[kind] + "_out"), c + 2)
                            o = psum[BANK[kind]][:]
                            w, half = kind[:-1], int(kind[-1])
                            cols = slice(half * 512, (half + 1) * 512)
                            pe.matmul(o, h_hi[par][:], wT_hi[w][:, cols], start=True, stop=False)
                            pe.matmul(o, h_hi[par][:], wT_lo[w][:, cols], start=False, stop=False)
                            pe.matmul(o, h_lo[par][:], wT_hi[w][:, cols], start=False, stop=True).then_inc(sem(kind + "_in"), 1)

                        def features_T(kind, c, par):
                            k, half = kind[1], int(kind[2])
                            if half:
                                pe.wait_ge(sem(f"t{k}0_out"), c + 1)
                            else:
                                pe.wait_ge(sem("a2_out" if k == "k" else "a3_out"), c)
                            pe.wait_ge(sem(f"phi_{k}_ready"), c + 1)
                            for j in range(4):
                                t = half * 4 + j
                                mm = pe.transpose(psum[BANK[kind]][:, j * P:(j + 1) * P], phi[k][par][:, t * P:(t + 1) * P], ident[:])
                            mm.then_inc(sem(kind + "_in"), 1)

                        def score(half, c):
                            for z in range(2):
                                pe.wait_ge(sem(f"a{z}_out" if half else f"t{'kq'[z]}1_out"), c + 1)
                            pe.wait_ge(sem(f"tk{half}_out"), c + 1)
                            pe.wait_ge(sem(f"tq{half}_out"), c + 1)
                            for j in range(4):
                                for z in range(2):
                                    r, kind = slice(z * M, (z + 1) * M), f"a{2 * half + z}"
                                    mm = pe.matmul(psum[BANK[kind]][:, j * P:(j + 1) * P], phiT["k"][r, half * 4 + j, :],
                                                   phiT["q"][r, half * 4 + j, :], start=True, stop=True)
                                    if j == 3:
                                        mm.then_inc(sem(kind + "_in"), 1)

                        def attend(g, c, par):
                            kind = f"o{g}"
                            if g < 2:
                                pe.wait_ge(sem(f"attT{g}_out"), c)
                            else:
                                pe.wait_ge(sem(f"o{g - 2}_out"), c + 1)
                            pe.wait_ge(sem("state_kept" if par == 0 else "kv2_out"), times(c + 1 - par))
                            for z in range(2):
                                pe.wait_ge(sem(f"a{g // 2 * 2 + z}_out"), c + 1)
                            for q in range(2):
                                p = g * 2 + q
                                pe.matmul(psum[BANK[kind]][:, q * PW:(q + 1) * PW], phiT["q"][:, p, :], state[par][:, p, :],
                                          start=(q == 0), stop=False, skip_group_check=True)
                                for z in range(2):
                                    h = 2 * p + z
                                    mm = pe.matmul(psum[BANK[kind]][:, q * PW + z * VW:q * PW + (z + 1) * VW],
                                                   scores[:, (p // 4 * 2 + z) * 4 + p % 4, :], v_sb[par][:, h, :], start=False,
                                                   stop=(q == 1 and z == 1), skip_group_check=True)
                            mm.then_inc(sem(kind + "_in"), 1)

                        def state_gain(g, c, par):
                            kind = f"kv{g}"
                            pe.wait_ge(sem(f"kv{(g - 1) % 3}_out"), c + min(g, 1))
                            for q, p in enumerate(KV_PAIRS[g]):
                                mm = pe.matmul(psum[BANK[kind]][:, q * PW:(q + 1) * PW], phi["k"][par][:, p * P:(p + 1) * P],
                                               v_sb[par][:, 2 * p:2 * p + 2, :].rearrange("p a b -> p (a b)"),
                                               start=True, stop=True)
                            mm.then_inc(sem(kind + "_in"), 1)

                        def attended_T(half, c):
                            kind = f"attT{half}"
                            pe.wait_ge(sem(f"o{2 * half + 1}_out"), c)
                            pe.wait_ge(sem(f"o{2 + half}_out"), c)
                            for j in range(4):
                                t = half * 4 + j
                                mm = pe.transpose(psum[BANK[kind]][:, j * P:(j + 1) * P],
                                                  att[:, 2 * t:2 * t + 2, :].rearrange("p a b -> p (a b)"), ident[:])
                            mm.then_inc(sem(kind + "_in"), 1)

                        def step(c, par):
                            nxt = 1 - par
                            front, back, tail = live(c, 1), live(c), live(c, -1)
                            last = live(c, -2)
                            if last:
                                pe.wait_ge(sem("hT_out"), times(c + 2, NCH))
                                pe.wait_ge(sem("h2_ready"), c - 1)
                                pe.transpose(psum[7][:, 0:P], h2_cur[par][:], ident[:]).then_inc(sem("h2T_in"), 1)
                            if back:
                                features_T("tk0", c, par)
                                features_T("tq0", c, par)
                            if front:
                                pe.wait_ge(sem("h_split"), c + 2)
                                project("q0", c, nxt)
                                project("q1", c, nxt)
                            if last:
                                pe.wait_ge(sem("h2T_out"), c - 1)
                                pe.matmul(psum[7][:, 0:E], h2T[:], wg_sb[:], start=True, stop=True).then_inc(sem("lg_in"), 1)
                            if back:
                                features_T("tk1", c, par)
                                features_T("tq1", c, par)
                            if front:
                                project("k0", c, nxt)
                                project("k1", c, nxt)
                            if back:
                                score(0, c)
                            if tail:
                                attended_T(0, c)
                                attended_T(1, c)
                            if front:
                                project("pq0", c, nxt)
                                project("pq1", c, nxt)
                            if back:
                                score(1, c)
                            if tail:
                                if last:
                                    pe.wait_ge(sem("lg_out"), c - 1)
                                else:
                                    pe.wait_ge(sem("hT_out"), times(c + 2, NCH))
                                pe.wait_ge(sem("attT0_out"), c)
                                pe.wait_ge(sem("attT1_out"), c)
                                for t in range(NP):
                                    mm = pe.matmul(psum[7][:, 0:D], attT[:, t, :], woT[:, t, :], start=(t == 0), stop=(t == NP - 1))
                                mm.then_inc(sem("wo_in"), 1)
                            if front:
                                project("pk0", c, nxt)
                                project("pk1", c, nxt)
                            if back:
                                pe.wait_ge(sem("v0_out"), c + 1)
                                pe.wait_ge(sem("v1_out"), c + 1)
                                state_gain(0, c, par)
                                attend(0, c, par)
                            if front:
                                project("v0", c, nxt)
                            if back:
                                attend(1, c, par)
                            if front:
                                project("v1", c, nxt)
                            if live(c, 2):
                                if tail:
                                    pe.wait_ge(sem("wo_out"), c)
                                else:
                                    pe.wait_ge(sem("hT_out"), times(c + 2))
                                pe.wait_ge(sem("xn_ready"), c + 3)
                                pe.transpose(psum[7][:, 0:P], xn[par][:], ident[:]).then_inc(sem("hT_in"), 1)
                            if back:
                                attend(2, c, par)
                                state_gain(1, c, par)
                                attend(3, c, par)
                                state_gain(2, c, par)
                        on_steps(pe, step)

                    @block.scalar
                    def _(act):
                        def step(c, par):
                            nxt = 1 - par
                            front, back, tail = live(c, 1), live(c), live(c, -1)

                            def features_T_out(half):
                                for k, bank in (("k", 2), ("q", 3)):
                                    act.wait_ge(sem(f"t{k}{half}_in"), c + 1)
                                    act.activation(phiT[k][:, half * 4:half * 4 + 4, :].rearrange("p a b -> p (a b)"),
                                                   psum[bank][:], ACT.Copy, scale=FEATURE_SCALE).then_inc(sem(f"t{k}{half}_out"), 1)

                            def squares(k):
                                act.wait_ge(sem(f"norm_{k}_ready"), c + 1)
                                for half in range(2):
                                    act.wait_ge(sem(f"{k}{half}_in"), c + 2)
                                    act.activation(square[k][:, half * 512:(half + 1) * 512], psum[half][:],
                                                   ACT.Square).then_inc(sem(f"{k}{half}_out"), 1)

                            def exps(k):
                                act.wait_ge(sem(f"p{k}0_out"), c + 2)
                                act.wait_ge(sem(f"p{k}1_out"), c + 2)
                                act.wait_ge(sem("tq1_in" if k == "q" else "kv2_in"), times(c))
                                act.activation(phi[k][nxt][:], expo[k][:], ACT.Exp).then_inc(sem(f"phi_{k}_ready"), 1)

                            last = live(c, -2)
                            if last:
                                act.wait_ge(sem("h2T_in"), c - 1)
                                act.copy(h2T[:], psum[7][:, 0:P]).then_inc(sem("h2T_out"), 1)
                            if back:
                                features_T_out(0)
                            if front:
                                squares("q")
                            if last:
                                act.wait_ge(sem("lg_in"), c - 1)
                                apart(act)
                                act.copy(logits[:, bass.ds((c - 2) * E, E)], psum[7][:, 0:E]).then_inc(sem("lg_out"), 1)
                            if back:
                                features_T_out(1)
                            if front:
                                squares("k")
                            if tail:
                                for half in range(2):
                                    act.wait_ge(sem(f"attT{half}_in"), c)
                                    act.copy(attT[:, half * 4:half * 4 + 4, :].rearrange("p a b -> p (a b)"),
                                             psum[4 + half][:]).then_inc(sem(f"attT{half}_out"), 1)
                            if front:
                                exps("q")
                                exps("k")
                                for half in range(2):
                                    act.wait_ge(sem(f"v{half}_in"), c + 2)
                                    act.wait_ge(sem("kv2_in"), times(c))
                                    act.copy(v_sb[nxt][:, half * 8:half * 8 + 8, 0:DH],
                                             psum[half][:].rearrange("p (h d) -> p h d", d=DH)).then_inc(sem(f"v{half}_out"), 1)
                            if live(c, 2):
                                act.wait_ge(sem("hT_in"), c + 3)
                                act.wait_ge(sem("h_split"), c + 2)
                                b = (c + 2) >> SHIFT
                                apart(act)
                                act.activation(h_full[:], psum[7][:, 0:P], ACT.Identity, bias=sa_col[:, bass.ds(b, 1)],
                                               scale=ca_col[:, bass.ds(b, 1)]).then_inc(sem("h_full_ready"), 1)
                                act.wait_ge(sem("v1_in"), times(c + 1))
                                apart(act)
                                act.activation(h_hi[par][:], psum[7][:, 0:P], ACT.Identity, bias=sa_col[:, bass.ds(b, 1)],
                                               scale=ca_col[:, bass.ds(b, 1)]).then_inc(sem("hT_out"), 1)
                        on_steps(act, step)

                    @block.vector
                    def _(dve):
                        def moments(tag, src, st, mv, var, n):
                            apart(dve)
                            dve.bn_stats(st[:], src).then_inc(sem(tag + "_stats"), 1)
                            dve.wait_ge(sem(tag + "_stats"), n)
                            apart(dve)
                            dve.bn_aggr(mv[:], st[:]).then_inc(sem(tag + "_aggr"), 1)
                            dve.wait_ge(sem(tag + "_aggr"), n)
                            dve.tensor_scalar(var[:], mv[:, 1:2], 1e-5, None, ALU.add).then_inc(sem(tag + "_var"), 1)

                        def first_moments(n):
                            dve.wait_ge(sem("xn_ready"), n)
                            moments("ln1", x_sb[:, bass.ds(n * D, D)], st1, mv1, var1, n + 1)

                        def first_norm(n, par):
                            dve.wait_ge(sem("hT_in"), times(n - 1))
                            dve.wait_ge(sem("ln1_rstd"), n + 1)
                            dve.tensor_scalar(xn[par][:], x_sb[:, bass.ds(n * D, D)], mv1[:, 0:1], rs1[:, 0:1],
                                              ALU.subtract, ALU.mult).then_inc(sem("xn_ready"), 1)

                        for i in range(2):
                            dve.memset(v_sb[i][:, :, DH:VW], 1.0)
                            dve.memset(state[i][:], 0.0).then_inc(sem("state_zeroed"), 1)
                        dve.wait_ge(sem("state_zeroed"), 2)
                        first_moments(0)
                        first_norm(0, 0)

                        def step(c, par):
                            nxt = 1 - par
                            front, back, tail = live(c, 1), live(c), live(c, -1)

                            def mask(g):
                                dve.wait_ge(sem(f"a{g}_in"), c + 1)
                                dve.tensor_tensor(scores[:, g * 4:g * 4 + 4, :], psum[BANK[f"a{g}"]][:].rearrange("p (h t) -> p h t", t=P),
                                                  causal[:], ALU.mult).then_inc(sem(f"a{g}_out"), 1)

                            def sum_squares(k):
                                dve.wait_ge(sem(f"{k}1_out"), c + 2)
                                dve.tensor_reduce(norm[k][:], square[k][:].rearrange("p (h d) -> p h d", d=DH), AX,
                                                  ALU.add).then_inc(sem(f"norm_{k}_ready"), 1)

                            def exponent(k):
                                dve.wait_ge(sem(f"norm_{k}_ready"), c + 2)
                                dve.wait_ge(sem(f"phi_{k}_ready"), c + 1)
                                for half in range(2):
                                    dve.wait_ge(sem(f"p{k}{half}_in"), c + 2)
                                    ins = dve.scalar_tensor_tensor(
                                        out=expo[k][:, half * 512:(half + 1) * 512].rearrange("p (h m) -> p h m", m=M),
                                        in0=norm[k][:, half * 8:half * 8 + 8].unsqueeze(2).to_broadcast([P, 8, M]), scalar=-0.5,
                                        in1=psum[half][:].rearrange("p (h m) -> p h m", m=M), op0=ALU.mult, op1=ALU.add)
                                    ins.then_inc(sem(f"p{k}{half}_out"), 1)

                            def normalise(g):
                                kind = f"o{g}"
                                o = psum[BANK[kind]][:, 0:2 * PW].rearrange("p (h w) -> p h w", w=VW)
                                dve.wait_ge(sem(kind + "_in"), c + 1)
                                dve.tensor_scalar(den[g % 2][:].unsqueeze(2), o[:, :, DH:VW], 1e-6, None, ALU.add).then_inc(sem(f"den{g % 2}"), 1)
                                dve.wait_ge(sem(f"den{g % 2}"), 2 * c + 1 + g // 2)
                                dve.reciprocal(rden[g % 2][:], den[g % 2][:]).then_inc(sem(f"rden{g % 2}"), 1)
                                dve.wait_ge(sem(f"rden{g % 2}"), 2 * c + 1 + g // 2)
                                dve.tensor_tensor(att[:, g * 4:g * 4 + 4, :], o[:, :, 0:DH],
                                                  rden[g % 2][:].unsqueeze(2).to_broadcast([P, 4, DH]), ALU.mult)\
                                   .then_inc(sem(kind + "_out"), 1)

                            def state_add(g):
                                kind = f"kv{g}"
                                dve.wait_ge(sem(kind + "_in"), c + 1)
                                n = len(KV_PAIRS[g])
                                p0 = KV_PAIRS[g][0]
                                gain = psum[6][:, 0:n * PW].rearrange("p (a w) -> p a w", w=PW)
                                for z in range(2):
                                    r, w = slice(z * M, (z + 1) * M), slice(z * VW, (z + 1) * VW)
                                    ins = dve.scalar_tensor_tensor(
                                        out=state[nxt][r, p0:p0 + n, w], in0=gain[r, :, w], scalar=FEATURE_SCALE,
                                        in1=state[par][r, p0:p0 + n, w], op0=ALU.mult, op1=ALU.add)
                                ins.then_inc(sem(kind + "_out"), 1)

                            if back and par == 0:
                                dve.wait_ge(sem("kv2_out"), c)
                                st = state[par][:].bitcast(U32)
                                dve.tensor_scalar(st, st, keep[:, bass.ds(c, 1)], None, ALU.bitwise_and)\
                                   .then_inc(sem("state_kept"), 2)
                            if front:
                                sum_squares("q")
                            if back:
                                mask(0)
                                mask(1)
                            if front:
                                exponent("q")
                            if live(c, 3):
                                first_moments(c + 3)
                            if front:
                                sum_squares("k")
                            if back:
                                mask(2)
                                mask(3)
                            if tail:
                                n = c - 1
                                b = n >> SHIFT
                                xs = x_sb[:, bass.ds(n * D, D)]
                                dve.wait_ge(sem("wo_in"), c)
                                dve.tensor_tensor(upd[0][:], psum[7][:, 0:D], bo_b[:], ALU.add).then_inc(sem("wo_out"), 1)
                                dve.wait_ge(sem("wo_out"), c)
                                dve.tensor_tensor(upd[1][:], upd[0][:], ga_b[:, bass.ds(b * D, D)], ALU.mult).then_inc(sem("gated"), 1)
                                dve.wait_ge(sem("gated"), c)
                                dve.tensor_tensor(xs, xs, upd[1][:], ALU.add).then_inc(sem("x2_ready"), 1)
                                dve.wait_ge(sem("x2_ready"), c)
                                moments("ln2", xs, st2, mv2, var2, c)
                            if front:
                                exponent("k")
                            if tail:
                                dve.wait_ge(sem("ln2_rstd"), c)
                                dve.tensor_scalar(xn2[:], xs, mv2[:, 0:1], rs2[:, 0:1], ALU.subtract, ALU.mult).then_inc(sem("xn2"), 1)
                                dve.wait_ge(sem("xn2"), c)
                                dve.tensor_tensor(xm2[:], xn2[:], cb_b[:, bass.ds(b * D, D)], ALU.mult).then_inc(sem("xm2"), 1)
                                dve.wait_ge(sem("xm2"), c)
                                dve.wait_ge(sem(f"h2_stored{nxt}"), times(16 * ((c + 1) >> 1)))
                                dve.wait_ge(sem("h2T_in"), times(c - 1))
                                dve.tensor_tensor(h2_cur[nxt][:], xm2[:], sb_b[:, bass.ds(b * D, D)], ALU.add).then_inc(sem("h2_ready"), 1)
                            if back:
                                state_add(0)
                                normalise(0)
                                normalise(1)
                            if live(c, 3):
                                first_norm(c + 3, nxt)
                            if back:
                                normalise(2)
                            if live(c, 2):
                                dve.wait_ge(sem("h_full_ready"), c + 3)
                                dve.wait_ge(sem("hT_out"), c + 3)
                                dve.tensor_tensor(h_lo[par][:], h_full[:], h_hi[par][:].bitcast(F32), ALU.subtract).then_inc(sem("h_split"), 1)
                            if back:
                                state_add(1)
                                normalise(3)
                                state_add(2)
                        on_steps(dve, step)

                    @block.gpsimd
                    def _(pool):
                        pool.memset(power[:], -0.5).then_inc(sem("power_set"), 1)
                        pool.wait_ge(sem("power_set"), 1)

                        def rstd(tag, var, rs, n):
                            pool.wait_ge(sem(tag + "_var"), n)
                            pool.tensor_tensor(rs[:], var[:], power[:], ALU.pow).then_inc(sem(tag + "_rstd"), 1)
                        rstd("ln1", var1, rs1, 1)

                        def step(c, par):
                            if live(c, 3):
                                rstd("ln1", var1, rs1, c + 4)
                            if live(c, -1):
                                rstd("ln2", var2, rs2, c)
                        on_steps(pool, step)

                    @block.sync
                    def _(sp):
                        def step(c, par):
                            if live(c, -1):
                                sp.wait_ge(sem("h2_ready"), c)
                                sp.dma_start(h2_rows[bass.ds((c - 1) * P, P), :], h2_cur[1 - par][:]).then_inc(sem(f"h2_stored{1 - par}"), 16)
                        for par in range(2):
                            sp.sem_inc(sem(f"h2_stored{par}"), 16)
                        on_steps(sp, step)
                        for par in range(2):
                            sp.wait_ge(sem(f"h2_stored{par}"), 16 * (NCH // 2 + 1))

        KV_PAIRS = [(0, 1, 2), (3, 4, 5), (6, 7)]
        h2_cur = [sb(f"h2_cur{i}", [P, D]) for i in range(2)]
        attention()

        gather_id = sb("gather_id", [P, NSL], I32)
        scatter_id = sb("scatter_id", [P, NSL], I32)
        weight = sb("weight", [P, KC])

        def routing():
            with ExitStack() as tmp:
                def tsb(name, shape, dt=F32):
                    return tmp.enter_context(nc.sbuf_tensor(name, shape, dt))
                top = tsb("top", [P, NCH])
                prob = tsb("prob", [P, NCH, E])
                total = tsb("total", [P, NCH])
                rest = tsb("rest", [P, NCH, E])
                hit = tsb("hit", [P, NCH, E])
                first = tsb("first", [P, NCH])
                chosen = tsb("chosen", [P, KC, E], BF16)
                PAD = KC // 2
                run = [tsb(f"run{i}", [P, PAD + KC, E]) for i in range(2)]
                place = tsb("place", [P, KC, E])
                pos = tsb("pos", [P, KC])
                kept = tsb("kept", [P, KC])
                expert = tsb("expert", [P, KC])
                pos_i = tsb("pos_i", [P, KC], I32)
                row_i = tsb("row_i", [P, KC], I32)
                tile_i = tsb("tile_i", [P, KC], I32)
                row_f = tsb("row_f", [P, KC])
                tile_f = tsb("tile_f", [P, KC])
                row_hot = tsb("row_hot", [P, KC, P], BF16)
                tile_hot = tsb("tile_hot", [P, KC, NSL], BF16)
                tagged = tsb("tagged", [P, KC, 2, NSL], BF16)
                slot_f = tsb("slot_f", [P, NSL])
                empty = tsb("empty", [P, NSL])
                m2_sb = tsb("m2_sb", [P, NSL])
                iota_p = tsb("iota_p", [P, P])
                iota_s = tsb("iota_s", [P, NSL])
                iota_e = tsb("iota_e", [P, E])
                rev_e = tsb("rev_e", [P, E])
                iota_kc = tsb("iota_kc", [P, KC])
                part = tsb("part", [P, 1])
                tri = tsb("tri", [P, P], BF16)
                ones = tsb("ones", [P, P], BF16)
                lg = logits[:].rearrange("p (c e) -> p c e", e=E)

                def wide(ap, n):
                    return ap.unsqueeze(2).to_broadcast([P, ap.shape[1], n])

                def tall(ap, n):
                    return ap.unsqueeze(1).to_broadcast([P, n, ap.shape[1]])

                with nc.Block() as block:
                    @block.gpsimd
                    def _(pool):
                        def iota(t, step, base, mult=0):
                            nc.gpsimd.iota(t[:], pattern=[[step, t.shape[1]]], base=base, channel_multiplier=mult,
                                           allow_small_or_imprecise_dtypes=True).then_inc(sem("iotas"), 1)
                        iota(iota_p, 1, 0)
                        iota(iota_s, 1, 0)
                        iota(iota_e, 1, 0)
                        iota(rev_e, -1, E)
                        iota(iota_kc, 1, 1)
                        iota(part, 1, 0, 1)
                        nc.gpsimd.memset(ones[:], 1.0).then_inc(sem("iotas"), 1)
                        nc.gpsimd.tensor_copy(tri[:], causal[:, 0, :]).then_inc(sem("iotas"), 1)

                    @block.scalar
                    def _(act):
                        act.wait_ge(sem("shifted"), 1)
                        act.activation(prob[:], rest[:], ACT.Exp).then_inc(sem("prob_exp"), 1)

                    @block.tensor
                    def _(pe):
                        pe.wait_ge(sem("iotas"), 8)
                        pe.wait_ge(sem("chosen_ready"), 1)
                        ch = chosen[:].rearrange("p a e -> p (a e)")
                        pe.matmul(psum[0][:], tri[:], ch, start=True, stop=True).then_inc(sem("counts"), 1)
                        pe.matmul(psum[1][:], ones[:], ch, start=True, stop=True).then_inc(sem("counts"), 1)
                        pe.wait_ge(sem("tagged_ready"), 1)
                        for a in range(KC):
                            mm = pe.matmul(psum[2][:, 0:2 * NSL], row_hot[:, a, :], tagged[:, a].rearrange("p a b -> p (a b)"),
                                           start=(a == 0), stop=(a == KC - 1))
                        mm.then_inc(sem("slots_filled"), 1)

                    @block.vector
                    def _(dve):
                        n = [0]

                        def link(ins):
                            n[0] += 1
                            ins.then_inc(sem("route_chain"), 1)
                            dve.wait_ge(sem("route_chain"), n[0])
                        dve.wait_ge(sem("iotas"), 8)
                        for i in range(2):
                            dve.memset(run[i][:, 0:PAD, :], 0.0)
                        link(dve.tensor_reduce(top[:], lg, AX, ALU.max))
                        dve.tensor_tensor(rest[:], lg, wide(top[:], E), ALU.subtract).then_inc(sem("shifted"), 1)
                        for k in range(2):
                            src = lg if k == 0 else rest[:]
                            if k:
                                link(dve.tensor_reduce(top[:], src, AX, ALU.max))
                            link(dve.tensor_tensor(hit[:], src, wide(top[:], E), ALU.is_equal))
                            link(dve.tensor_tensor(hit[:], hit[:], tall(rev_e[:], NCH), ALU.mult))
                            link(dve.tensor_reduce(first[:], hit[:], AX, ALU.max))
                            link(dve.tensor_tensor(chosen[:, k * NCH:(k + 1) * NCH, :], tall(rev_e[:], NCH), wide(first[:], E), ALU.is_equal))
                            if k == 0:
                                dve.wait_ge(sem("prob_exp"), 1)
                                link(dve.scalar_tensor_tensor(out=rest[:], in0=chosen[:, 0:NCH, :], scalar=-3e38, in1=lg,
                                                              op0=ALU.mult, op1=ALU.add))
                        dve.engine_nop().then_inc(sem("chosen_ready"), 1)
                        link(dve.tensor_reduce(total[:], prob[:], AX, ALU.add))
                        link(dve.reciprocal(total[:], total[:]))
                        link(dve.tensor_tensor(prob[:], prob[:], wide(total[:], E), ALU.mult))
                        for k in range(2):
                            link(dve.tensor_tensor(hit[:], prob[:], chosen[:, k * NCH:(k + 1) * NCH, :], ALU.mult))
                            link(dve.tensor_reduce(weight[:, k * NCH:(k + 1) * NCH], hit[:], AX, ALU.add))
                        link(dve.tensor_tensor(total[:], weight[:, 0:NCH], weight[:, NCH:KC], ALU.add))
                        link(dve.tensor_scalar(total[:], total[:], 1e-9, None, ALU.max))
                        link(dve.reciprocal(total[:], total[:]))
                        for k in range(2):
                            w = weight[:, k * NCH:(k + 1) * NCH]
                            link(dve.tensor_tensor(w, w, total[:], ALU.mult))
                        dve.wait_ge(sem("counts"), 2)
                        link(dve.tensor_copy(run[0][:, PAD:, :].rearrange("p a e -> p (a e)"), psum[1][:]))
                        a, shift = 0, 1
                        while shift < KC:
                            link(dve.tensor_tensor(run[1 - a][:, PAD:, :], run[a][:, PAD:, :],
                                                   run[a][:, PAD - shift:PAD - shift + KC, :], ALU.add))
                            a, shift = 1 - a, shift * 2
                        flat = place[:].rearrange("p a e -> p (a e)")
                        link(dve.tensor_tensor(flat, run[a][:, PAD:, :].rearrange("p a e -> p (a e)"), psum[1][:], ALU.subtract))
                        link(dve.tensor_tensor(flat, flat, psum[0][:], ALU.add))
                        link(dve.tensor_tensor(place[:], place[:], chosen[:], ALU.mult))
                        link(dve.tensor_reduce(pos[:], place[:], AX, ALU.add))
                        link(dve.tensor_scalar(pos[:], pos[:], -1.0, None, ALU.add))
                        link(dve.tensor_tensor(place[:], chosen[:], tall(iota_e[:], KC), ALU.mult))
                        link(dve.tensor_reduce(expert[:], place[:], AX, ALU.add))
                        link(dve.tensor_scalar(kept[:], pos[:], float(CAP), None, ALU.is_lt))
                        link(dve.tensor_tensor(weight[:], weight[:], kept[:], ALU.mult))
                        link(dve.tensor_copy(pos_i[:], pos[:]))
                        link(dve.tensor_scalar(row_i[:], pos_i[:], P - 1, None, ALU.bitwise_and))
                        link(dve.tensor_scalar(tile_i[:], pos_i[:], P.bit_length() - 1, None, ALU.logical_shift_right))
                        link(dve.tensor_copy(row_f[:], row_i[:]))
                        link(dve.tensor_copy(tile_f[:], tile_i[:]))
                        link(dve.scalar_tensor_tensor(out=tile_f[:], in0=expert[:], scalar=float(TPE), in1=tile_f[:],
                                                      op0=ALU.mult, op1=ALU.add))
                        link(dve.tensor_scalar(kept[:], kept[:], -1000.0, 1000.0, ALU.mult, ALU.add))
                        link(dve.tensor_tensor(tile_f[:], tile_f[:], kept[:], ALU.add))
                        dve.tensor_tensor(row_hot[:], tall(iota_p[:], KC), wide(row_f[:], P), ALU.is_equal)
                        link(dve.tensor_tensor(tile_hot[:], tall(iota_s[:], KC), wide(tile_f[:], NSL), ALU.is_equal))
                        dve.tensor_tensor(tagged[:, :, 0, :], tile_hot[:], wide(iota_kc[:], NSL), ALU.mult)
                        dve.tensor_scalar(tagged[:, :, 1, :], tile_hot[:], part[:, 0:1], None, ALU.mult).then_inc(sem("tagged_ready"), 1)
                        dve.wait_ge(sem("slots_filled"), 1)
                        link(dve.tensor_copy(m2_sb[:], psum[2][:, NSL:2 * NSL]))
                        link(dve.scalar_tensor_tensor(out=slot_f[:], in0=psum[2][:, 0:NSL], scalar=float(P), in1=m2_sb[:],
                                                      op0=ALU.mult, op1=ALU.add))
                        link(dve.tensor_scalar(empty[:], psum[2][:, 0:NSL], 0.0, float(SKIP), ALU.is_equal, ALU.mult))
                        link(dve.scalar_tensor_tensor(out=scatter_id[:], in0=slot_f[:], scalar=-float(P), in1=empty[:],
                                                      op0=ALU.add, op1=ALU.add))
                        link(dve.tensor_scalar(gather_id[:], slot_f[:], -float(P), 0.0, ALU.add, ALU.max))
                        link(dve.tensor_scalar(gather_id[:], gather_id[:], N - 1, None, ALU.bitwise_and))
        routing()

        def experts():
            with ExitStack() as tmp:
                def tsb(name, shape, dt=F32):
                    return tmp.enter_context(nc.sbuf_tensor(name, shape, dt))
                GW = GS * P
                rows = [tsb(f"rows{i}", [P, GS, D]) for i in range(2)]
                rowsT_hi = [tsb(f"rowsT_hi{i}", [P, GW], F32R) for i in range(2)]
                rowsT_lo = [tsb(f"rowsT_lo{i}", [P, GW], F32R) for i in range(2)]
                hidden = [tsb(f"hidden{i}", [P, KH, GW]) for i in range(2)]
                y_sb = [tsb(f"y_sb{i}", [P, GS, D]) for i in range(2)]
                g_now = [tsb(f"g_now{i}", [P, GS], I32) for i in range(2)]
                s_now = [tsb(f"s_now{i}", [P, GS], I32) for i in range(2)]
                w1_nat = [tsb(f"w1_nat{i}", [P, HID]) for i in range(2)]
                w1_hi = [tsb(f"w1_hi{i}", [P, HID], F32R) for i in range(2)]
                w1_lo = [tsb(f"w1_lo{i}", [P, HID], F32R) for i in range(2)]
                w2_sb = [tsb(f"w2_sb{i}", [P, KH, D]) for i in range(2)]
                w1_rows = w1.rearrange("e d h -> (e d) h")
                w2_rows = w2.rearrange("e (k p) d -> p (e k) d", p=P)
                GPE = TPE // GS
                BODY = 2 * GPE

                def on_groups(eng, step):
                    for j in range(BODY):
                        step(j, j, j // GPE)
                    with eng.Fori(1, NG // BODY) as i:
                        for j in range(BODY):
                            step(i * BODY + j, j, i * 2 + j // GPE)

                with nc.Block() as block:
                    @block.sync
                    def _(sp):
                        def step(g, j, e):
                            if j % GPE:
                                return
                            par = j // GPE
                            sp.wait_ge(sem("w1_split"), times(e - 1))
                            sp.dma_start(w1_nat[par][:], w1_rows[bass.ds(e * P, P), :]).then_inc(sem(f"w1_in{par}"), 16)
                            sp.wait_ge(sem("y_in"), times(g - 2))
                            sp.dma_start(w2_sb[par][:], w2_rows[:, bass.ds(e * KH, KH), :]).then_inc(sem(f"w2_in{par}"), 16)
                        on_groups(sp, step)

                    @block.gpsimd
                    def _(pool):
                        def gather(g, par):
                            pool.wait_ge(sem("rowsT_in"), times(g - 1))
                            pool.wait_ge(sem(f"rows_in{par}"), times((g >> 1) * 16 * GS))
                            apart(pool)
                            pool.tensor_copy(g_now[par][:], gather_id[:, bass.ds(g * GS, GS)]).then_inc(sem("g_now"), 1)
                            pool.wait_ge(sem("g_now"), g + 1)
                            apart(pool)
                            for t in range(GS):
                                pool.indirect_dma_start(
                                    out=rows[par][:, t, :], out_offset=None, in_=h2_rows[:, :],
                                    in_offset=bass.IndirectOffsetOnAxis(ap=g_now[par][:, t:t + 1].bitcast(U32), axis=0),
                                ).then_inc(sem(f"rows_in{par}"), 16)

                        def scatter(g, par):
                            pool.wait_ge(sem("y_out"), g + 1)
                            pool.wait_ge(sem(f"y_stored{par}"), times((g >> 1) * 16 * GS))
                            apart(pool)
                            pool.tensor_copy(s_now[par][:], scatter_id[:, bass.ds(g * GS, GS)]).then_inc(sem("s_now"), 1)
                            pool.wait_ge(sem("s_now"), g + 1)
                            apart(pool)
                            for t in range(GS):
                                pool.indirect_dma_start(
                                    out=y_rows[:, :], out_offset=bass.IndirectOffsetOnAxis(ap=s_now[par][:, t:t + 1].bitcast(U32), axis=0),
                                    in_=y_sb[par][:, t, :], in_offset=None, bounds_check=2 * N - 1, oob_is_err=False,
                                ).then_inc(sem(f"y_stored{par}"), 16)
                        def step(g, j, e):
                            gather(g, j % 2)
                            if not isinstance(g, int) or g >= 2:
                                scatter(g - 2, j % 2)
                        on_groups(pool, step)
                        scatter(NG - 2, 0)
                        scatter(NG - 1, 1)
                        for par in range(2):
                            pool.wait_ge(sem(f"y_stored{par}"), NG // 2 * 16 * GS)

                    @block.tensor
                    def _(pe):
                        def down(g, par, w):
                            pe.wait_ge(sem(f"w2_in{w}"), times(((g >> 2) + 1) * 16))
                            pe.wait_ge(sem("hid3_out"), g + 1)
                            pe.wait_ge(sem("y_out"), times(g - 1))
                            for t in range(GS):
                                for k in range(KH):
                                    mm = pe.matmul(psum[6 + par][:, t * D:(t + 1) * D], hidden[par][:, k, t * P:(t + 1) * P],
                                                   w2_sb[w][:, k, :], start=(k == 0), stop=(k == KH - 1))
                            mm.then_inc(sem("y_in"), 1)

                        def step(g, j, e):
                            par, w = j % 2, j // GPE
                            pe.wait_ge(sem(f"rows_in{par}"), times(((g >> 1) + 1) * 16 * GS))
                            pe.wait_ge(sem("rowsT_split"), times(g - 1))
                            for t in range(GS):
                                mm = pe.transpose(psum[par][:, t * P:(t + 1) * P], rows[par][:, t, :], ident[:])
                            mm.then_inc(sem("rowsT_in"), 1)
                            if not isinstance(g, int) or g >= 1:
                                down(g - 1, 1 - par, ((j - 1) % BODY) // GPE)
                            pe.wait_ge(sem("rowsT_split"), g + 1)
                            pe.wait_ge(sem("w1_split"), times((g >> 1) + 1))
                            for k in range(KH):
                                pe.wait_ge(sem(f"hid{k}_out"), g)
                                o, ks = psum[2 + k][:], slice(k * P, (k + 1) * P)
                                pe.matmul(o, w1_hi[w][:, ks], rowsT_hi[par][:], start=True, stop=False)
                                pe.matmul(o, w1_lo[w][:, ks], rowsT_hi[par][:], start=False, stop=False)
                                pe.matmul(o, w1_hi[w][:, ks], rowsT_lo[par][:], start=False, stop=True).then_inc(sem(f"hid{k}_in"), 1)
                        on_groups(pe, step)
                        down(NG - 1, 1, 1)

                    @block.scalar
                    def _(act):
                        def step(g, j, e):
                            par = j % 2
                            act.wait_ge(sem("rowsT_in"), g + 1)
                            act.wait_ge(sem("hid3_in"), times(g - 1))
                            act.copy(rowsT_hi[par][:], psum[par][:]).then_inc(sem("rowsT_hi_done"), 1)
                            act.wait_ge(sem("y_in"), times(g - 1))
                            for k in range(KH):
                                act.wait_ge(sem(f"hid{k}_in"), g + 1)
                                apart(act)
                                act.activation(hidden[par][:, k, :], psum[2 + k][:], ACT.Gelu,
                                               bias=b1_col[:, bass.ds(e * KH + k, 1)]).then_inc(sem(f"hid{k}_out"), 1)
                        on_groups(act, step)

                    @block.vector
                    def _(dve):
                        def y_out(g, par, e):
                            dve.wait_ge(sem("y_in"), g + 1)
                            dve.wait_ge(sem(f"y_stored{par}"), times((g >> 1) * 16 * GS))
                            dve.tensor_tensor(y_sb[par][:], psum[6 + par][:].rearrange("p (t d) -> p t d", d=D),
                                              b2_b[:, bass.ds(e * D, D)].unsqueeze(1).to_broadcast([P, GS, D]), ALU.add)\
                               .then_inc(sem("y_out"), 1)

                        def step(g, j, e):
                            par, w = j % 2, j // GPE
                            if j % GPE == 0:
                                dve.wait_ge(sem(f"w1_in{w}"), times(((g >> 2) + 1) * 16))
                                dve.wait_ge(sem("hid3_in"), times(g - 2))
                                dve.tensor_copy(w1_hi[w][:], w1_nat[w][:]).then_inc(sem("w1_hi_done"), 1)
                                dve.wait_ge(sem("w1_hi_done"), times((g >> 1) + 1))
                                dve.tensor_tensor(w1_lo[w][:], w1_nat[w][:], w1_hi[w][:].bitcast(F32), ALU.subtract).then_inc(sem("w1_split"), 1)
                            dve.wait_ge(sem("rowsT_hi_done"), g + 1)
                            dve.tensor_tensor(rowsT_lo[par][:], psum[par][:], rowsT_hi[par][:].bitcast(F32), ALU.subtract).then_inc(sem("rowsT_split"), 1)
                            if not isinstance(g, int) or g >= 1:
                                y_out(g - 1, 1 - par, e if j % GPE else e - 1)
                        on_groups(dve, step)
                        y_out(NG - 1, 1, E - 1)
        experts()

        def combine():
            with ExitStack() as tmp:
                def tsb(name, shape, dt=F32):
                    return tmp.enter_context(nc.sbuf_tensor(name, shape, dt))
                y = [[tsb(f"y{k}_{i}", [P, CPB, D]) for i in range(2)] for k in range(2)]
                y_v = y_rows.rearrange("(a p) d -> p a d", p=P)
                with nc.Block() as block:
                    @block.sync
                    def _(sp):
                        for b in range(B):
                            for k in range(2):
                                sp.wait_ge(sem("out_ready" if k == 0 else "combine_step"), times(b - 1 if k == 0 else 3 * (b - 2) + 2))
                                sp.dma_start(y[k][b % 2][:], y_v[:, k * NCH + b * CPB:k * NCH + (b + 1) * CPB, :]).then_inc(sem(f"y{k}_loaded{b % 2}"), 16)

                    @block.gpsimd
                    def _(pool):
                        for b in range(B):
                            t = y[1][b % 2]
                            pool.wait_ge(sem(f"y1_loaded{b % 2}"), 16 * (b // 2 + 1))
                            pool.tensor_tensor(t[:], t[:], weight[:, NCH + b * CPB:NCH + (b + 1) * CPB].unsqueeze(2).to_broadcast([P, CPB, D]),
                                               ALU.mult).then_inc(sem("scaled1"), 1)

                    @block.vector
                    def _(dve):
                        for b in range(B):
                            t = y[0][b % 2]
                            xs = x_sb[:, b * CPB * D:(b + 1) * CPB * D].rearrange("p (c d) -> p c d", d=D)
                            dve.wait_ge(sem(f"y0_loaded{b % 2}"), 16 * (b // 2 + 1))
                            dve.tensor_tensor(t[:], t[:], weight[:, b * CPB:(b + 1) * CPB].unsqueeze(2).to_broadcast([P, CPB, D]),
                                              ALU.mult).then_inc(sem("combine_step"), 1)
                            dve.wait_ge(sem("combine_step"), 3 * b + 1)
                            dve.wait_ge(sem("scaled1"), b + 1)
                            dve.tensor_tensor(t[:], t[:], y[1][b % 2][:], ALU.add).then_inc(sem("combine_step"), 1)
                            dve.wait_ge(sem("combine_step"), 3 * b + 2)
                            dve.tensor_tensor(t[:], t[:], gb_b[:, b * D:(b + 1) * D].unsqueeze(1).to_broadcast([P, CPB, D]),
                                              ALU.mult).then_inc(sem("combine_step"), 1)
                            dve.wait_ge(sem("combine_step"), 3 * b + 3)
                            dve.tensor_tensor(xs, xs, t[:], ALU.add).then_inc(sem("out_ready"), 1)

                    @block.scalar
                    def _(act):
                        for b in range(B):
                            act.wait_ge(sem("out_ready"), b + 1)
                            act.dma_start(out_v[:, b * CPB:(b + 1) * CPB, :],
                                          x_sb[:, b * CPB * D:(b + 1) * CPB * D].rearrange("p (c d) -> p c d", d=D)).then_inc(sem("out_stored"), 16)
                        act.wait_ge(sem("out_stored"), 16 * B)
        combine()


_INS = ["L0_attn_x", "L0_attn_omega", "L0_attn_wq", "L0_attn_wk", "L0_attn_wv", "L0_attn_wo", "L0_attn_bo",
        "L0_ffn_wg", "L0_ffn_w1", "L0_ffn_b1", "L0_ffn_w2", "L0_ffn_b2", "L0_c", "L0_wmod"]
_OUTS = [((4, 1024, 128), "float32")]


def kernel(**inputs):
    import numpy as _np
    import concourse.bacc as _bacc
    from concourse import mybir as _mybir
    from concourse.bass_utils import run_bass_kernel_spmd as _run

    nc = _bacc.Bacc("TRN2", target_bir_lowering=False, num_devices=1)
    arrays, args = {}, []
    for name in _INS:
        a = _np.ascontiguousarray(inputs[name])
        arrays[f"in_{name}_dram"] = a
        args.append(nc.dram_tensor(f"in_{name}_dram", a.shape, _mybir.dt.from_np(a.dtype), kind="ExternalInput").ap())
    for i, (shape, dtype) in enumerate(_OUTS):
        dt = _mybir.dt.from_np(_np.dtype(dtype))
        args.append(nc.dram_tensor(f"out_{i}_dram", shape, dt, kind="ExternalOutput").ap())
    build(nc, *args)
    r = _run(nc, [arrays], core_ids=[0])
    got = tuple(r.results[0][f"out_{i}_dram"] for i in range(len(_OUTS)))
    return got[0]
```

```python
from contextlib import ExitStack

import concourse.bass as bass
from concourse import mybir

F32 = mybir.dt.float32
F32R = mybir.dt.float32r
BF16 = mybir.dt.bfloat16
I32 = mybir.dt.int32
U32 = mybir.dt.uint32
ALU = mybir.AluOpType
ACT = mybir.ActivationFunctionType
AX = mybir.AxisListType.X

P = 128


def build(nc, x, omega, wq, wk, wv, wo, bo, wg, w1, b1, w2, b2, cond, wmod, out):
    B, S, D = x.shape
    M, DH = omega.shape
    HD = wq.shape[0]
    H = HD // DH
    NP = H // 2
    E, _, HID = w1.shape
    KH = HID // P
    N = B * S
    NCH = N // P
    CPB = S // P
    SHIFT = CPB.bit_length() - 1
    CAP = (2 * N + E - 1) // E
    NSL = E * CAP // P
    TPE = CAP // P
    GS = 4
    NG = NSL // GS
    RW = D + 1
    BLANK = 8
    VW = DH + 1
    PW = 2 * VW
    SKIP = 200000
    FEATURE_SCALE = float(M) ** -0.5
    assert D == P and DH == 64 and M == 64 and E == 8 and CAP % (GS * P) == 0 and HD == 1024

    dispatched = nc.dram_tensor("dispatched", [2 * E * CAP, RW], F32, kind="Internal").ap()
    y_rows = nc.dram_tensor("y_rows", [2 * N, D], F32, kind="Internal").ap()

    with ExitStack() as ctx:
        def sb(name, shape, dt=F32):
            return ctx.enter_context(nc.sbuf_tensor(name, shape, dt))

        sems = {}

        def sem(name):
            if name not in sems:
                sems[name] = ctx.enter_context(nc.semaphore(name))
            return sems[name]

        def times(count, most=None):
            if not isinstance(count, int):
                return count
            return max(count, 0) if most is None else min(max(count, 0), most)

        def apart(eng):
            eng.sem_inc(sem("wait_passed"), 1)

        x_sb = sb("x_sb", [P, NCH * D])
        wT_hi = {k: sb(f"w{k}_hi", [P, HD], F32R) for k in ("q", "k", "v", "pq", "pk")}
        wT_lo = {k: sb(f"w{k}_lo", [P, HD], F32R) for k in ("q", "k", "v", "pq", "pk")}
        woT = sb("woT", [P, NP, D])
        wg_sb = sb("wg_sb", [P, E])
        ident = sb("ident", [P, P])
        causal = sb("causal", [P, 4, P])
        keep = sb("keep", [P, NCH], U32)
        sa_col = sb("sa_col", [P, B + 1])
        ca_col = sb("ca_col", [P, B + 1])
        ga_b = sb("ga_b", [P, (B + 1) * D])
        sb_b = sb("sb_b", [P, (B + 1) * D])
        cb_b = sb("cb_b", [P, (B + 1) * D])
        gb_b = sb("gb_b", [P, (B + 1) * D])
        bo_b = sb("bo_b", [P, D])
        b2_b = sb("b2_b", [P, E * D])
        b1_col = sb("b1_col", [P, E * KH])
        top_logits = sb("top_logits", [P, NCH * E])
        token = sb("token", [P, NCH])
        iota_e = sb("iota_e", [P, E])
        first_limit = sb("first_limit", [P, E])
        second_limit = sb("second_limit", [P, E])
        taken = sb("taken", [P, 2 * E])
        sign = sb("sign", [P, 2])
        slot_number = sb("slot_number", [P, NSL])
        weight = sb("weight", [P, NCH, 2])
        tri = sb("tri", [P, P], BF16)
        ones = sb("ones", [P, P], BF16)
        blank = [sb(f"blank{i}", [P, BLANK, RW]) for i in range(2)]
        w1_nat = [sb(f"w1_nat{i}", [P, HID]) for i in range(2)]
        w2_sb = [sb(f"w2_sb{i}", [P, KH, D]) for i in range(2)]
        w1_rows = w1.rearrange("e d h -> (e d) h")
        w2_rows = w2.rearrange("e (k p) d -> p (e k) d", p=P)

        psum = [ctx.enter_context(nc.psum_tensor(f"bank{i}", [P, 512], F32)) for i in range(8)]

        x_v = x.rearrange("b (c p) d -> p (b c) d", p=P)
        out_v = out.rearrange("b (c p) d -> p (b c) d", p=P)

        def setup():
            with ExitStack() as tmp:
                def tsb(name, shape, dt=F32):
                    return tmp.enter_context(nc.sbuf_tensor(name, shape, dt))
                w_nat = {k: tsb(f"w{k}_nat", [P, NP, D]) for k in ("q", "k", "v")}
                wo_nat = tsb("wo_nat", [P, HD])
                om_blk = tsb("om_blk", [P, P])
                omT_blk = tsb("omT_blk", [P, P])
                c_nat = tsb("c_nat", [B, D])
                c_sig = tsb("c_sig", [B, D])
                c_silu = tsb("c_silu", [B, D])
                siluT = tsb("siluT", [P, B])
                silu_b = tsb("silu_b", [P, B, P])
                wmod_sb = tsb("wmod_sb", [P, 6 * D])
                b1_nat = tsb("b1_nat", [E * KH, P])
                sgn = tsb("sgn", [P, B * D])
                mag = tsb("mag", [P, B * D])
                with nc.Block() as block:
                    @block.sync
                    def _(sp):
                        sp.dma_start(wo_nat[:], wo).then_inc(sem("wo_loaded"), 16)
                        for k, w in (("q", wq), ("k", wk), ("v", wv)):
                            sp.dma_start(w_nat[k][:], w.rearrange("(j p) d -> p j d", p=P)).then_inc(sem("qkv_loaded"), 16)
                        sp.dma_start(b1_nat[:], b1.rearrange("e (k p) -> (e k) p", p=P)).then_inc(sem("s_b1"), 16)
                        sp.wait_ge(sem("om_zeroed"), 1)
                        for i in range(2):
                            sp.dma_start(om_blk[i * M:(i + 1) * M, i * DH:(i + 1) * DH], omega).then_inc(sem("s_om"), 16)
                        for i in range(4):
                            n = NCH // 4
                            sp.dma_start(x_sb[:, i * n * D:(i + 1) * n * D].rearrange("p (c d) -> p c d", d=D),
                                         x_v[:, i * n:(i + 1) * n, :]).then_inc(sem("later_loads"), 16)
                        sp.wait_ge(sem("blank_ready"), 1)
                        for region in range(2):
                            for i in range(E * CAP // (P * BLANK)):
                                r0 = region * E * CAP + i * P * BLANK
                                sp.dma_start(dispatched[r0:r0 + P * BLANK, :].rearrange("(p r) d -> p (r d)", p=P),
                                             blank[region][:].rearrange("p r d -> p (r d)")).then_inc(sem("dispatched_blank"), 16)
                        for i in range(2 * N // (P * BLANK)):
                            sp.dma_start(y_rows[i * P * BLANK:(i + 1) * P * BLANK, :].rearrange("(p r) d -> p (r d)", p=P),
                                         blank[0][:].rearrange("p r d -> p (r d)")[:, 0:BLANK * D]).then_inc(sem("y_zeroed"), 16)

                    @block.scalar
                    def _(act):
                        act.dma_start(c_nat[:], cond).then_inc(sem("s_c"), 16)
                        act.dma_start(wmod_sb[:], wmod).then_inc(sem("s_wmod"), 16)
                        act.dma_start(wg_sb[:], wg).then_inc(sem("later_loads"), 16)
                        act.dma_start(bo_b[:], bo.rearrange("(a d) -> a d", a=1).to_broadcast([P, D])).then_inc(sem("later_loads"), 16)
                        act.dma_start(b2_b[:], b2.rearrange("(a e) d -> a (e d)", a=1).to_broadcast([P, E * D])).then_inc(sem("later_loads"), 16)
                        act.wait_ge(sem("s_c"), 16)
                        nc.scalar.activation(c_sig[:], c_nat[:], ACT.Exp, scale=-1.0).then_inc(sem("c_exp"), 1)
                        for n, (k, half) in enumerate(WEIGHTS):
                            act.wait_ge(sem("wT_filled"), n + 1)
                            nc.scalar.copy(wT_hi[k][:, half * 512:(half + 1) * 512], psum[n % 4][:]).then_inc(sem("wT_hi_done"), 1)

                    @block.gpsimd
                    def _(pool):
                        nc.gpsimd.memset(om_blk[:], 0.0).then_inc(sem("om_zeroed"), 1)
                        nc.gpsimd.memset(ident[:], 0.0).then_inc(sem("p_chain"), 1)
                        nc.gpsimd.memset(causal[:], 1.0).then_inc(sem("p_chain"), 1)
                        pool.wait_ge(sem("p_chain"), 2)
                        nc.gpsimd.affine_select(out=ident[:], in_=ident[:], compare_op=ALU.not_equal, fill=1.0, base=0,
                                                pattern=[[-1, P]], channel_multiplier=1).then_inc(sem("ident_ready"), 1)
                        nc.gpsimd.affine_select(out=causal[:], in_=causal[:], compare_op=ALU.is_ge, fill=0.0, base=0,
                                                pattern=[[0, 4], [1, P]], channel_multiplier=-1).then_inc(sem("p_chain"), 1)
                        for i in range(2):
                            nc.gpsimd.memset(blank[i][:], 0.0).then_inc(sem("p_chain"), 1)
                        pool.wait_ge(sem("p_chain"), 5)
                        nc.gpsimd.memset(blank[1][:, :, D:RW], float(SKIP)).then_inc(sem("blank_ready"), 1)
                        nc.gpsimd.tensor_copy(tri[:], causal[:, 0, :]).then_inc(sem("tables"), 1)
                        nc.gpsimd.memset(ones[:], 1.0).then_inc(sem("tables"), 1)
                        nc.gpsimd.memset(sign[:, 0:1], 1.0).then_inc(sem("tables"), 1)
                        nc.gpsimd.memset(sign[:, 1:2], -1.0).then_inc(sem("tables"), 1)

                        def iota(t, step, base, mult=0):
                            nc.gpsimd.iota(t, pattern=[[step, t.shape[1]]], base=base, channel_multiplier=mult,
                                           allow_small_or_imprecise_dtypes=True).then_inc(sem("tables"), 1)
                        iota(token[:], P, 0, 1)
                        iota(slot_number[:], P, 0, 1)
                        iota(iota_e[:], 1, 0)
                        iota(first_limit[:], CAP, CAP - 1)
                        iota(second_limit[:], CAP, E * CAP)
                        iota(taken[:, 0:E], CAP, -1)
                        iota(taken[:, E:2 * E], CAP, (E + 1) * CAP)
                        pool.wait_ge(sem("tables"), 11)

                    @block.tensor
                    def _(pe):
                        pe.wait_ge(sem("ident_ready"), 1)
                        pe.wait_ge(sem("s_om"), 32)
                        pe.transpose(psum[7][:, 0:P], om_blk[:], ident[:]).then_inc(sem("small_filled"), 1)
                        pe.wait_ge(sem("silu_ready"), 1)
                        pe.wait_ge(sem("small_used"), 1)
                        pe.transpose(psum[7][:, 0:B], c_silu[:], ident[0:B, 0:B]).then_inc(sem("small_filled"), 1)
                        pe.wait_ge(sem("small_used"), 2)
                        pe.wait_ge(sem("s_b1"), 16)
                        pe.transpose(psum[7][:, 0:E * KH], b1_nat[:], ident[0:E * KH, 0:E * KH]).then_inc(sem("small_filled"), 1)
                        for n, (k, half) in enumerate(WEIGHTS):
                            if n >= 4:
                                pe.wait_ge(sem("wT_split"), times(n - 3))
                            dst = psum[n % 4]
                            src = w_nat[k[-1]]
                            pe.wait_ge(sem("qkv_loaded"), 48)
                            for j in range(4):
                                t = half * 4 + j
                                o = dst[:, j * P:(j + 1) * P]
                                if k in "qkv":
                                    mm = pe.transpose(o, src[:, t, :], ident[:])
                                else:
                                    mm = pe.matmul(o, src[:, t, :], omT_blk[:], start=True, stop=True)
                            mm.then_inc(sem("wT_filled"), 1)
                        pe.wait_ge(sem("wo_loaded"), 16)
                        for half in range(2):
                            for j in range(4):
                                t = half * 4 + j
                                mm = pe.transpose(psum[4 + half][:, j * P:(j + 1) * P], wo_nat[:, t * P:(t + 1) * P], ident[:])
                            mm.then_inc(sem("woT_filled"), 1)
                        pe.wait_ge(sem("s_wmod"), 16)
                        pe.wait_ge(sem("small_used"), 3)
                        pe.matmul(psum[7][:, 0:B], wmod_sb[:, 0:D], siluT[:], start=True, stop=True)
                        pe.matmul(psum[7][:, 64:64 + B], wmod_sb[:, D:2 * D], siluT[:], start=True, stop=True).then_inc(sem("mod_filled"), 1)
                        for m in range(4):
                            pe.wait_ge(sem("mod_used"), m)
                            for b in range(B):
                                mm = pe.matmul(psum[6][:, b * D:(b + 1) * D], silu_b[:, b, :],
                                               wmod_sb[:, (2 + m) * D:(3 + m) * D], start=True, stop=True)
                            mm.then_inc(sem("mod_filled"), 1)

                    @block.vector
                    def _(dve):
                        dve_n = [0]

                        def link(ins):
                            dve_n[0] += 1
                            ins.then_inc(sem("d_chain"), 1)
                            dve.wait_ge(sem("d_chain"), dve_n[0])
                        link(dve.memset(keep[:], 0xFFFFFFFF))
                        link(dve.memset(keep[:].rearrange("p (b c) -> p b c", c=CPB)[:, :, 0:1], 0))
                        dve.wait_ge(sem("small_filled"), 1)
                        dve.tensor_copy(omT_blk[:], psum[7][:, 0:P]).then_inc(sem("small_used"), 1)
                        dve.wait_ge(sem("c_exp"), 1)
                        link(dve.tensor_scalar(c_sig[:], c_sig[:], 1.0, None, ALU.add))
                        link(dve.reciprocal(c_sig[:], c_sig[:]))
                        dve.tensor_tensor(c_silu[:], c_nat[:], c_sig[:], ALU.mult).then_inc(sem("silu_ready"), 1)
                        dve.wait_ge(sem("small_filled"), 2)
                        link(dve.tensor_copy(siluT[:], psum[7][:, 0:B]))
                        dve.tensor_copy(silu_b[:], siluT[:].unsqueeze(2).to_broadcast([P, B, P])).then_inc(sem("small_used"), 1)
                        dve.wait_ge(sem("small_filled"), 3)
                        dve.tensor_copy(b1_col[:], psum[7][:, 0:E * KH]).then_inc(sem("small_used"), 1)
                        for n, (k, half) in enumerate(WEIGHTS):
                            dve.wait_ge(sem("wT_hi_done"), n + 1)
                            cols = slice(half * 512, (half + 1) * 512)
                            dve.tensor_tensor(wT_lo[k][:, cols], psum[n % 4][:], wT_hi[k][:, cols].bitcast(F32),
                                              ALU.subtract).then_inc(sem("wT_split"), 1)
                        for half in range(2):
                            dve.wait_ge(sem("woT_filled"), half + 1)
                            link(dve.tensor_copy(woT[:, half * 4:half * 4 + 4, :].rearrange("p j d -> p (j d)"), psum[4 + half][:]))
                        dve.wait_ge(sem("mod_filled"), 1)
                        link(dve.tensor_copy(sa_col[:, 0:B], psum[7][:, 0:B]))
                        link(dve.tensor_scalar(ca_col[:, 0:B], psum[7][:, 64:64 + B], 1.0, None, ALU.add))
                        for m, t in enumerate((ga_b, sb_b, cb_b, gb_b)):
                            dve.wait_ge(sem("mod_filled"), m + 2)
                            if t is sb_b:
                                dve.tensor_copy(t[:, 0:B * D], psum[6][:]).then_inc(sem("mod_used"), 1)
                            elif t is cb_b:
                                dve.tensor_scalar(t[:, 0:B * D], psum[6][:], 1.0, None, ALU.add).then_inc(sem("mod_used"), 1)
                            else:
                                link(dve.tensor_scalar(sgn[:], psum[6][:], 0.0, 2.0, ALU.is_ge, ALU.mult))
                                link(dve.tensor_scalar(mag[:], psum[6][:], -1.0, None, ALU.mult))
                                link(dve.tensor_tensor(mag[:], psum[6][:], mag[:], ALU.max))
                                link(dve.tensor_scalar(mag[:], mag[:], 0.25, None, ALU.max))
                                dve.scalar_tensor_tensor(out=t[:, 0:B * D], in0=sgn[:], scalar=-1.0, in1=mag[:],
                                                         op0=ALU.add, op1=ALU.mult).then_inc(sem("mod_used"), 1)
                        dve.wait_ge(sem("mod_used"), 4)
                        dve.wait_ge(sem("wT_split"), len(WEIGHTS))
                        dve.wait_ge(sem("later_loads"), 16 * 7)

        WEIGHTS = [(k, half) for k in ("q", "k", "v", "pq", "pk") for half in range(2)]
        setup()

        def attention():
            with ExitStack() as tmp:
                def tsb(name, shape, dt=F32):
                    return tmp.enter_context(nc.sbuf_tensor(name, shape, dt))
                xn = [tsb(f"xn{i}", [P, D]) for i in range(2)]
                st1 = tsb("st1", [P, 6])
                mv1 = tsb("mv1", [P, 2])
                rs1 = tsb("rs1", [P, 1])
                var1 = tsb("var1", [P, 1])
                var2 = tsb("var2", [P, 1])
                power = tsb("power", [P, 1])
                h_full = tsb("h_full", [P, P])
                h_hi = [tsb(f"h_hi{i}", [P, P], F32R) for i in range(2)]
                h_lo = [tsb(f"h_lo{i}", [P, P], F32R) for i in range(2)]
                square = {k: tsb(f"square_{k}", [P, HD]) for k in "qk"}
                norm = {k: tsb(f"norm_{k}", [P, H]) for k in "qk"}
                expo = {k: tsb(f"expo_{k}", [P, HD]) for k in "qk"}
                phi = {k: [tsb(f"phi_{k}{i}", [P, HD]) for i in range(2)] for k in "qk"}
                phiT = {k: tsb(f"phiT_{k}", [P, NP, P]) for k in "qk"}
                v_sb = [tsb(f"v_sb{i}", [P, H, VW]) for i in range(2)]
                scores = tsb("scores", [P, H, P])
                state = [tsb(f"state{i}", [P, NP, PW]) for i in range(2)]
                den = [tsb(f"den{i}", [P, 4]) for i in range(2)]
                rden = [tsb(f"rden{i}", [P, 4]) for i in range(2)]
                att = tsb("att", [P, H, DH])
                attT = tsb("attT", [P, NP, P])
                upd = [tsb(f"upd{i}", [P, D]) for i in range(2)]
                st2 = tsb("st2", [P, 6])
                mv2 = tsb("mv2", [P, 2])
                rs2 = tsb("rs2", [P, 1])
                x2_now = tsb("x2_now", [P, D])
                xn2 = tsb("xn2", [P, D])
                xm2 = tsb("xm2", [P, D])
                h2T = tsb("h2T", [P, P])
                lg_now = tsb("lg_now", [P, E])
                top = [tsb(f"top{i}", [P, E]) for i in range(2)]
                best = tsb("best", [P, E], U32)
                best_f = tsb("best_f", [P, 2])
                hot = tsb("hot", [P, 2 * E], BF16)
                place = tsb("place", [P, 2 * E])
                over = tsb("over", [P, 2 * E])
                slot_f = tsb("slot_f", [P, 2])
                slot = [tsb(f"slot{i}", [P, 2], I32) for i in range(2)]

                TURNS = {0: ["q0", "k0", "pq0", "pk0", "v0"], 1: ["q1", "k1", "pq1", "pk1", "v1"],
                         2: ["tk0", "tk1", "a0", "a2"], 3: ["tq0", "tq1", "a1", "a3"],
                         4: ["attT0", "o0", "o2"], 5: ["attT1", "o1", "o3"],
                         6: ["kv0", "kv1", "kv2"], 7: ["h2T", "lg", "rank", "wo", "hT"]}
                BANK = {k: b for b, ks in TURNS.items() for k in ks}
                BEFORE = {k: ks[i - 1] for ks in TURNS.values() for i, k in enumerate(ks)}

                def on_steps(eng, step):
                    for c in range(-2, 4):
                        step(c, c % 2)
                    with eng.Fori(2, NCH // 2 - 2) as i:
                        for j in range(2):
                            step(2 * i + j, j)
                    for c in range(NCH - 4, NCH + 2):
                        step(c, c % 2)

                def live(c, ahead=0):
                    return not isinstance(c, int) or 0 <= c + ahead < NCH

                with nc.Block() as block:
                    @block.tensor
                    def _(pe):
                        def project(kind, c, par):
                            if kind[:-1] == "q":
                                pe.wait_ge(sem(f"v{kind[-1]}_out"), times(c + 1))
                            else:
                                pe.wait_ge(sem(BEFORE[kind] + "_out"), c + 2)
                            o = psum[BANK[kind]][:]
                            w, half = kind[:-1], int(kind[-1])
                            cols = slice(half * 512, (half + 1) * 512)
                            pe.matmul(o, h_hi[par][:], wT_hi[w][:, cols], start=True, stop=False)
                            pe.matmul(o, h_hi[par][:], wT_lo[w][:, cols], start=False, stop=False)
                            pe.matmul(o, h_lo[par][:], wT_hi[w][:, cols], start=False, stop=True).then_inc(sem(kind + "_in"), 1)

                        def features_T(kind, c, par):
                            k, half = kind[1], int(kind[2])
                            if half:
                                pe.wait_ge(sem(f"t{k}0_out"), c + 1)
                            else:
                                pe.wait_ge(sem("a2_out" if k == "k" else "a3_out"), c)
                            pe.wait_ge(sem(f"phi_{k}_ready"), c + 1)
                            for j in range(4):
                                t = half * 4 + j
                                mm = pe.transpose(psum[BANK[kind]][:, j * P:(j + 1) * P], phi[k][par][:, t * P:(t + 1) * P], ident[:])
                            mm.then_inc(sem(kind + "_in"), 1)

                        def score(half, c):
                            for z in range(2):
                                pe.wait_ge(sem(f"a{z}_out" if half else f"t{'kq'[z]}1_out"), c + 1)
                            pe.wait_ge(sem(f"tk{half}_out"), c + 1)
                            pe.wait_ge(sem(f"tq{half}_out"), c + 1)
                            for j in range(4):
                                for z in range(2):
                                    r, kind = slice(z * M, (z + 1) * M), f"a{2 * half + z}"
                                    mm = pe.matmul(psum[BANK[kind]][:, j * P:(j + 1) * P], phiT["k"][r, half * 4 + j, :],
                                                   phiT["q"][r, half * 4 + j, :], start=True, stop=True)
                                    if j == 3:
                                        mm.then_inc(sem(kind + "_in"), 1)

                        def attend(g, c, par):
                            kind = f"o{g}"
                            if g < 2:
                                pe.wait_ge(sem(f"attT{g}_out"), c)
                            else:
                                pe.wait_ge(sem(f"o{g - 2}_out"), c + 1)
                            pe.wait_ge(sem("state_kept" if par == 0 else "kv2_out"), times(c + 1 - par))
                            for z in range(2):
                                pe.wait_ge(sem(f"a{g // 2 * 2 + z}_out"), c + 1)
                            for q in range(2):
                                p = g * 2 + q
                                pe.matmul(psum[BANK[kind]][:, q * PW:(q + 1) * PW], phiT["q"][:, p, :], state[par][:, p, :],
                                          start=(q == 0), stop=False, skip_group_check=True)
                                for z in range(2):
                                    h = 2 * p + z
                                    mm = pe.matmul(psum[BANK[kind]][:, q * PW + z * VW:q * PW + (z + 1) * VW],
                                                   scores[:, (p // 4 * 2 + z) * 4 + p % 4, :], v_sb[par][:, h, :], start=False,
                                                   stop=(q == 1 and z == 1), skip_group_check=True)
                            mm.then_inc(sem(kind + "_in"), 1)

                        def state_gain(g, c, par):
                            kind = f"kv{g}"
                            pe.wait_ge(sem(f"kv{(g - 1) % 3}_out"), c + min(g, 1))
                            for q, p in enumerate(KV_PAIRS[g]):
                                mm = pe.matmul(psum[BANK[kind]][:, q * PW:(q + 1) * PW], phi["k"][par][:, p * P:(p + 1) * P],
                                               v_sb[par][:, 2 * p:2 * p + 2, :].rearrange("p a b -> p (a b)"),
                                               start=True, stop=True)
                            mm.then_inc(sem(kind + "_in"), 1)

                        def attended_T(half, c):
                            kind = f"attT{half}"
                            pe.wait_ge(sem(f"o{2 * half + 1}_out"), c)
                            pe.wait_ge(sem(f"o{2 + half}_out"), c)
                            for j in range(4):
                                t = half * 4 + j
                                mm = pe.transpose(psum[BANK[kind]][:, j * P:(j + 1) * P],
                                                  att[:, 2 * t:2 * t + 2, :].rearrange("p a b -> p (a b)"), ident[:])
                            mm.then_inc(sem(kind + "_in"), 1)

                        def step(c, par):
                            nxt = 1 - par
                            front, back, tail = live(c, 1), live(c), live(c, -1)
                            last = live(c, -2)
                            if back:
                                features_T("tk0", c, par)
                                features_T("tq0", c, par)
                            if last:
                                pe.wait_ge(sem("hT_out"), times(c + 2, NCH))
                                pe.wait_ge(sem("h2_ready"), c - 1)
                                pe.transpose(psum[7][:, 0:P], h2_cur[par][:, 0:D], ident[:]).then_inc(sem("h2T_in"), 1)
                            if front:
                                pe.wait_ge(sem("h_split"), c + 2)
                                project("q0", c, nxt)
                                project("q1", c, nxt)
                            if last:
                                pe.wait_ge(sem("h2T_out"), c - 1)
                                pe.matmul(psum[7][:, 0:E], h2T[:], wg_sb[:], start=True, stop=True).then_inc(sem("lg_in"), 1)
                            if back:
                                features_T("tk1", c, par)
                                features_T("tq1", c, par)
                            if front:
                                project("k0", c, nxt)
                                project("k1", c, nxt)
                            if back:
                                score(0, c)
                            if tail:
                                attended_T(0, c)
                                attended_T(1, c)
                            if front:
                                project("pq0", c, nxt)
                                project("pq1", c, nxt)
                            if last:
                                pe.wait_ge(sem("lg_out"), c - 1)
                                pe.wait_ge(sem("hot_ready"), c - 1)
                                pe.matmul(psum[7][:, 0:2 * E], tri[:], hot[:], start=True, stop=True)
                                pe.matmul(psum[7][:, 2 * E:4 * E], ones[:], hot[:], start=True, stop=True).then_inc(sem("rank_in"), 1)
                            if back:
                                score(1, c)
                            if tail:
                                if last:
                                    pe.wait_ge(sem("rank_out"), c - 1)
                                else:
                                    pe.wait_ge(sem("hT_out"), times(c + 2, NCH))
                                pe.wait_ge(sem("attT0_out"), c)
                                pe.wait_ge(sem("attT1_out"), c)
                                for t in range(NP):
                                    mm = pe.matmul(psum[7][:, 0:D], attT[:, t, :], woT[:, t, :], start=(t == 0), stop=(t == NP - 1))
                                mm.then_inc(sem("wo_in"), 1)
                            if front:
                                project("pk0", c, nxt)
                                project("pk1", c, nxt)
                            if back:
                                pe.wait_ge(sem("v0_out"), c + 1)
                                pe.wait_ge(sem("v1_out"), c + 1)
                                state_gain(0, c, par)
                                attend(0, c, par)
                            if front:
                                project("v0", c, nxt)
                            if back:
                                attend(1, c, par)
                            if front:
                                project("v1", c, nxt)
                            if live(c, 2):
                                if tail:
                                    pe.wait_ge(sem("wo_out"), c)
                                else:
                                    pe.wait_ge(sem("hT_out"), times(c + 2))
                                pe.wait_ge(sem("xn_ready"), c + 3)
                                pe.transpose(psum[7][:, 0:P], xn[par][:], ident[:]).then_inc(sem("hT_in"), 1)
                            if back:
                                state_gain(1, c, par)
                                attend(2, c, par)
                                attend(3, c, par)
                                state_gain(2, c, par)
                        on_steps(pe, step)

                    @block.scalar
                    def _(act):
                        def step(c, par):
                            nxt = 1 - par
                            front, back, tail = live(c, 1), live(c), live(c, -1)

                            def features_T_out(half):
                                for k, bank in (("k", 2), ("q", 3)):
                                    act.wait_ge(sem(f"t{k}{half}_in"), c + 1)
                                    act.activation(phiT[k][:, half * 4:half * 4 + 4, :].rearrange("p a b -> p (a b)"),
                                                   psum[bank][:], ACT.Copy, scale=FEATURE_SCALE).then_inc(sem(f"t{k}{half}_out"), 1)

                            def squares(k):
                                act.wait_ge(sem(f"norm_{k}_ready"), c + 1)
                                for half in range(2):
                                    act.wait_ge(sem(f"{k}{half}_in"), c + 2)
                                    act.activation(square[k][:, half * 512:(half + 1) * 512], psum[half][:],
                                                   ACT.Square).then_inc(sem(f"{k}{half}_out"), 1)

                            def exps(k):
                                act.wait_ge(sem(f"p{k}0_out"), c + 2)
                                act.wait_ge(sem(f"p{k}1_out"), c + 2)
                                act.wait_ge(sem("tq1_in" if k == "q" else "kv2_in"), times(c))
                                act.activation(phi[k][nxt][:], expo[k][:], ACT.Exp).then_inc(sem(f"phi_{k}_ready"), 1)

                            last = live(c, -2)
                            if back:
                                features_T_out(0)
                            if last:
                                act.wait_ge(sem("h2T_in"), c - 1)
                                act.copy(h2T[:], psum[7][:, 0:P]).then_inc(sem("h2T_out"), 1)
                            if front:
                                squares("q")
                            if last:
                                act.wait_ge(sem("lg_in"), c - 1)
                                act.copy(lg_now[:], psum[7][:, 0:E]).then_inc(sem("lg_out"), 1)
                            if back:
                                features_T_out(1)
                            if front:
                                squares("k")
                            if tail:
                                for half in range(2):
                                    act.wait_ge(sem(f"attT{half}_in"), c)
                                    act.copy(attT[:, half * 4:half * 4 + 4, :].rearrange("p a b -> p (a b)"),
                                             psum[4 + half][:]).then_inc(sem(f"attT{half}_out"), 1)
                            if front:
                                exps("q")
                                exps("k")
                                for half in range(2):
                                    act.wait_ge(sem(f"v{half}_in"), c + 2)
                                    act.wait_ge(sem("kv2_in"), times(c))
                                    act.copy(v_sb[nxt][:, half * 8:half * 8 + 8, 0:DH],
                                             psum[half][:].rearrange("p (h d) -> p h d", d=DH)).then_inc(sem(f"v{half}_out"), 1)
                            if live(c, 2):
                                act.wait_ge(sem("hT_in"), c + 3)
                                act.wait_ge(sem("h_split"), c + 2)
                                b = (c + 2) >> SHIFT
                                apart(act)
                                act.activation(h_full[:], psum[7][:, 0:P], ACT.Identity, bias=sa_col[:, bass.ds(b, 1)],
                                               scale=ca_col[:, bass.ds(b, 1)])
                                act.wait_ge(sem("v1_in"), times(c + 1))
                                apart(act)
                                act.activation(h_hi[par][:], psum[7][:, 0:P], ACT.Identity, bias=sa_col[:, bass.ds(b, 1)],
                                               scale=ca_col[:, bass.ds(b, 1)]).then_inc(sem("hT_out"), 1)
                        on_steps(act, step)

                    @block.vector
                    def _(dve):
                        def moments(tag, src, st, mv, var, n):
                            apart(dve)
                            dve.bn_stats(st[:], src).then_inc(sem(tag + "_step"), 1)
                            dve.wait_ge(sem(tag + "_step"), 2 * n - 1)
                            apart(dve)
                            dve.bn_aggr(mv[:], st[:]).then_inc(sem(tag + "_step"), 1)
                            dve.wait_ge(sem(tag + "_step"), 2 * n)
                            dve.tensor_scalar(var[:], mv[:, 1:2], 1e-5, None, ALU.add).then_inc(sem(tag + "_var"), 1)

                        def first_moments(n):
                            dve.wait_ge(sem("xn_ready"), n)
                            moments("ln1", x_sb[:, bass.ds(n * D, D)], st1, mv1, var1, n + 1)

                        def first_norm(n, par):
                            dve.wait_ge(sem("hT_in"), times(n - 1))
                            dve.wait_ge(sem("ln1_rstd"), n + 1)
                            dve.tensor_scalar(xn[par][:], x_sb[:, bass.ds(n * D, D)], mv1[:, 0:1], rs1[:, 0:1],
                                              ALU.subtract, ALU.mult).then_inc(sem("xn_ready"), 1)

                        for i in range(2):
                            dve.memset(v_sb[i][:, :, DH:VW], 1.0)
                            dve.memset(state[i][:], 0.0).then_inc(sem("state_zeroed"), 1)
                        dve.wait_ge(sem("state_zeroed"), 2)
                        first_moments(0)
                        first_norm(0, 0)

                        def step(c, par):
                            nxt = 1 - par
                            front, back, tail = live(c, 1), live(c), live(c, -1)

                            def mask(g):
                                dve.wait_ge(sem(f"a{g}_in"), c + 1)
                                dve.tensor_tensor(scores[:, g * 4:g * 4 + 4, :], psum[BANK[f"a{g}"]][:].rearrange("p (h t) -> p h t", t=P),
                                                  causal[:], ALU.mult).then_inc(sem(f"a{g}_out"), 1)

                            def sum_squares(k):
                                dve.wait_ge(sem(f"{k}1_out"), c + 2)
                                dve.tensor_reduce(norm[k][:], square[k][:].rearrange("p (h d) -> p h d", d=DH), AX,
                                                  ALU.add).then_inc(sem(f"norm_{k}_ready"), 1)

                            def exponent(k):
                                dve.wait_ge(sem(f"norm_{k}_ready"), c + 2)
                                dve.wait_ge(sem(f"phi_{k}_ready"), c + 1)
                                for half in range(2):
                                    dve.wait_ge(sem(f"p{k}{half}_in"), c + 2)
                                    ins = dve.scalar_tensor_tensor(
                                        out=expo[k][:, half * 512:(half + 1) * 512].rearrange("p (h m) -> p h m", m=M),
                                        in0=norm[k][:, half * 8:half * 8 + 8].unsqueeze(2).to_broadcast([P, 8, M]), scalar=-0.5,
                                        in1=psum[half][:].rearrange("p (h m) -> p h m", m=M), op0=ALU.mult, op1=ALU.add)
                                    ins.then_inc(sem(f"p{k}{half}_out"), 1)

                            def normalise(g):
                                kind = f"o{g}"
                                o = psum[BANK[kind]][:, 0:2 * PW].rearrange("p (h w) -> p h w", w=VW)
                                dve.wait_ge(sem(kind + "_in"), c + 1)
                                dve.tensor_scalar(den[g % 2][:].unsqueeze(2), o[:, :, DH:VW], 1e-6, None, ALU.add).then_inc(sem("den_step"), 1)
                                dve.wait_ge(sem("den_step"), 8 * c + 2 * g + 1)
                                dve.reciprocal(rden[g % 2][:], den[g % 2][:]).then_inc(sem("den_step"), 1)
                                dve.wait_ge(sem("den_step"), 8 * c + 2 * g + 2)
                                dve.tensor_tensor(att[:, g * 4:g * 4 + 4, :], o[:, :, 0:DH],
                                                  rden[g % 2][:].unsqueeze(2).to_broadcast([P, 4, DH]), ALU.mult)\
                                   .then_inc(sem(kind + "_out"), 1)

                            def state_add(g):
                                kind = f"kv{g}"
                                dve.wait_ge(sem(kind + "_in"), c + 1)
                                n = len(KV_PAIRS[g])
                                p0 = KV_PAIRS[g][0]
                                gain = psum[6][:, 0:n * PW].rearrange("p (a w) -> p a w", w=PW)
                                for z in range(2):
                                    r, w = slice(z * M, (z + 1) * M), slice(z * VW, (z + 1) * VW)
                                    ins = dve.scalar_tensor_tensor(
                                        out=state[nxt][r, p0:p0 + n, w], in0=gain[r, :, w], scalar=FEATURE_SCALE,
                                        in1=state[par][r, p0:p0 + n, w], op0=ALU.mult, op1=ALU.add)
                                ins.then_inc(sem(kind + "_out"), 1)

                            def choose():
                                n = c - 1
                                dve.wait_ge(sem(f"sent{par}"), times(32 * ((c - 2) >> 1)))
                                dve.wait_ge(sem("lg_out"), n)
                                apart(dve)
                                dve.max(top[par][:], lg_now[:]).then_inc(sem("top_ready"), 1)
                                dve.wait_ge(sem("top_ready"), n)
                                apart(dve)
                                dve.max_index(best[:], top[par][:], lg_now[:]).then_inc(sem("choose_step"), 1)
                                dve.wait_ge(sem("choose_step"), 2 * n - 1)
                                dve.tensor_copy(best_f[:], best[:, 0:2]).then_inc(sem("choose_step"), 1)
                                dve.wait_ge(sem("choose_step"), 2 * n)
                                dve.tensor_scalar(hot[:, 0:E], iota_e[:], best_f[:, 0:1], None, ALU.is_equal)
                                dve.tensor_scalar(hot[:, E:2 * E], iota_e[:], best_f[:, 1:2], -1.0, ALU.is_equal, ALU.mult)\
                                   .then_inc(sem("hot_ready"), 1)

                            def find_slots():
                                n = c - 1
                                dve.wait_ge(sem("rank_in"), n)
                                dve.tensor_tensor(place[:], psum[7][:, 0:2 * E], taken[:], ALU.add).then_inc(sem("slot_step"), 1)
                                dve.tensor_tensor(taken[:], psum[7][:, 2 * E:4 * E], taken[:], ALU.add).then_inc(sem("rank_out"), 1)
                                dve.wait_ge(sem("slot_step"), 5 * n - 4)
                                dve.tensor_tensor(over[:, 0:E], place[:, 0:E], first_limit[:], ALU.is_gt)
                                dve.tensor_tensor(over[:, E:2 * E], place[:, E:2 * E], second_limit[:], ALU.is_lt).then_inc(sem("slot_step"), 1)
                                dve.wait_ge(sem("slot_step"), 5 * n - 3)
                                dve.scalar_tensor_tensor(out=place[:], in0=over[:], scalar=float(SKIP), in1=place[:],
                                                         op0=ALU.mult, op1=ALU.add).then_inc(sem("slot_step"), 1)
                                dve.wait_ge(sem("slot_step"), 5 * n - 2)
                                dve.tensor_tensor(place[:], place[:], hot[:], ALU.mult).then_inc(sem("slot_step"), 1)
                                dve.wait_ge(sem("slot_step"), 5 * n - 1)
                                dve.tensor_reduce(slot_f[:], place[:].rearrange("p (k e) -> p k e", e=E), AX, ALU.add).then_inc(sem("slot_step"), 1)
                                dve.wait_ge(sem("slot_step"), 5 * n)
                                dve.tensor_tensor(slot[par][:], slot_f[:], sign[:], ALU.mult).then_inc(sem("slot_ready"), 1)

                            if back and par == 0:
                                dve.wait_ge(sem("kv2_out"), c)
                                st = state[par][:].bitcast(U32)
                                dve.tensor_scalar(st, st, keep[:, bass.ds(c, 1)], None, ALU.bitwise_and)\
                                   .then_inc(sem("state_kept"), 2)
                            if front:
                                sum_squares("q")
                            if live(c, -2):
                                choose()
                            if back:
                                mask(0)
                                mask(1)
                            if front:
                                exponent("q")
                            if live(c, -2):
                                find_slots()
                            if live(c, 3):
                                first_moments(c + 3)
                            if front:
                                sum_squares("k")
                            if back:
                                mask(2)
                                mask(3)
                            if tail:
                                dve.wait_ge(sem("x2_ready"), times(c - 1))
                                dve.wait_ge(sem("wo_in"), c)
                                dve.tensor_tensor(upd[0][:], psum[7][:, 0:D], bo_b[:], ALU.add).then_inc(sem("wo_out"), 1)
                            if front:
                                exponent("k")
                            if tail:
                                dve.wait_ge(sem("x2_ready"), c)
                                moments("ln2", x2_now[:], st2, mv2, var2, c)
                            if back:
                                state_add(0)
                                normalise(0)
                                normalise(1)
                            if live(c, 3):
                                first_norm(c + 3, nxt)
                            if back:
                                state_add(1)
                                normalise(2)
                            if live(c, 2):
                                dve.wait_ge(sem("hT_out"), c + 3)
                                dve.tensor_tensor(h_lo[par][:], h_full[:], h_hi[par][:].bitcast(F32), ALU.subtract).then_inc(sem("h_split"), 1)
                            if back:
                                normalise(3)
                                state_add(2)
                        on_steps(dve, step)

                    @block.gpsimd
                    def _(pool):
                        pool.memset(power[:], -0.5).then_inc(sem("power_set"), 1)
                        pool.wait_ge(sem("power_set"), 1)

                        def rstd(tag, var, rs, n):
                            pool.wait_ge(sem(tag + "_var"), n)
                            pool.tensor_tensor(rs[:], var[:], power[:], ALU.pow).then_inc(sem(tag + "_rstd"), 1)
                        rstd("ln1", var1, rs1, 1)

                        def step(c, par):
                            nxt = 1 - par
                            if live(c, -2):
                                n = c - 2
                                pool.wait_ge(sem("top_ready"), c - 1)
                                apart(pool)
                                pool.tensor_copy(top_logits[:, bass.ds(n * E, E)], top[par][:])
                                pool.wait_ge(sem("slot_ready"), c - 1)
                                apart(pool)
                                for k in range(2):
                                    pool.indirect_dma_start(
                                        out=dispatched[:, :], in_=h2_cur[par][:], in_offset=None,
                                        out_offset=bass.IndirectOffsetOnAxis(ap=slot[par][:, k:k + 1].bitcast(U32), axis=0),
                                        bounds_check=2 * E * CAP - 1, oob_is_err=False).then_inc(sem(f"sent{par}"), 16)
                            if live(c, 3):
                                rstd("ln1", var1, rs1, c + 4)
                            if live(c, -1):
                                n = c - 1
                                b = n >> SHIFT
                                xs = x_sb[:, bass.ds(n * D, D)]
                                pool.wait_ge(sem("wo_out"), c)
                                apart(pool)
                                pool.tensor_tensor(upd[1][:], upd[0][:], ga_b[:, bass.ds(b * D, D)], ALU.mult).then_inc(sem("norm2_step"), 1)
                                pool.wait_ge(sem("norm2_step"), 3 * c - 2)
                                apart(pool)
                                pool.tensor_tensor(x2_now[:], xs, upd[1][:], ALU.add).then_inc(sem("x2_ready"), 1)
                                pool.wait_ge(sem("x2_ready"), c)
                                apart(pool)
                                pool.tensor_copy(xs, x2_now[:])
                                rstd("ln2", var2, rs2, c)
                                pool.wait_ge(sem("ln2_rstd"), c)
                                apart(pool)
                                pool.tensor_scalar(xn2[:], x2_now[:], mv2[:, 0:1], rs2[:, 0:1], ALU.subtract, ALU.mult).then_inc(sem("norm2_step"), 1)
                                pool.wait_ge(sem("norm2_step"), 3 * c - 1)
                                apart(pool)
                                pool.tensor_tensor(xm2[:], xn2[:], cb_b[:, bass.ds(b * D, D)], ALU.mult).then_inc(sem("norm2_step"), 1)
                                pool.wait_ge(sem("norm2_step"), 3 * c)
                                pool.wait_ge(sem(f"sent{nxt}"), times(32 * (n >> 1)))
                                pool.wait_ge(sem("h2T_in"), times(c - 2))
                                apart(pool)
                                pool.tensor_copy(h2_cur[nxt][:, D:RW], token[:, bass.ds(n, 1)])
                                pool.tensor_tensor(h2_cur[nxt][:, 0:D], xm2[:], sb_b[:, bass.ds(b * D, D)], ALU.add).then_inc(sem("h2_ready"), 1)
                            if isinstance(c, int) and c == 1:
                                pool.wait_ge(sem("dispatched_blank"), 16 * (2 * E * CAP // (P * BLANK)))
                        on_steps(pool, step)
                        for par in range(2):
                            pool.wait_ge(sem(f"sent{par}"), 16 * NCH)

                    @block.sync
                    def _(sp):
                        for e in range(2):
                            sp.dma_start(w1_nat[e][:], w1_rows[e * P:(e + 1) * P, :]).then_inc(sem(f"w1_in{e}"), 16)
                            sp.dma_start(w2_sb[e][:], w2_rows[:, e * KH:(e + 1) * KH, :]).then_inc(sem(f"w2_in{e}"), 16)

        KV_PAIRS = [(0, 1, 2), (3, 4, 5), (6, 7)]
        h2_cur = [sb(f"h2_cur{i}", [P, RW]) for i in range(2)]
        attention()

        def experts():
            with ExitStack() as tmp:
                def tsb(name, shape, dt=F32):
                    return tmp.enter_context(nc.sbuf_tensor(name, shape, dt))
                GW = GS * P
                region = [[tsb(f"region{k}_{i}", [P, GS, RW]) for i in range(2)] for k in range(2)]
                rows = [tsb(f"rows{i}", [P, GS, RW]) for i in range(2)]
                rowsT_hi = [tsb(f"rowsT_hi{i}", [P, GW], F32R) for i in range(2)]
                rowsT_lo = [tsb(f"rowsT_lo{i}", [P, GW], F32R) for i in range(2)]
                hidden = [tsb(f"hidden{i}", [P, KH, GW]) for i in range(2)]
                y_sb = [tsb(f"y_sb{i}", [P, GS, D]) for i in range(2)]
                row_id = [tsb(f"row_id{i}", [P, GS], I32) for i in range(4)]
                w1_hi = [tsb(f"w1_hi{i}", [P, HID], F32R) for i in range(2)]
                w1_lo = [tsb(f"w1_lo{i}", [P, HID], F32R) for i in range(2)]
                second = tsb("second", [P, NSL])
                shifted = tsb("shifted", [P, NCH, E])
                prob = tsb("prob", [P, NCH, E])
                total = tsb("total", [P, NCH])
                slot_rows = dispatched.rearrange("(a p) d -> p a d", p=P)
                GPE = TPE // GS
                BODY = 2 * GPE

                def on_groups(eng, step):
                    for j in range(BODY):
                        step(j, j, j // GPE)
                    with eng.Fori(1, NG // BODY - 1) as i:
                        for j in range(BODY):
                            step(i * BODY + j, j, i * 2 + j // GPE)
                    for j in range(BODY):
                        step(NG - BODY + j, j, E - 2 + j // GPE)

                def at_least(n, least):
                    return not isinstance(n, int) or n >= least

                def exists(e):
                    return not isinstance(e, int) or e < E

                with nc.Block() as block:
                    @block.sync
                    def _(sp):
                        def step(g, j, e):
                            par, w = j % 2, j // GPE
                            sp.wait_ge(sem("rows_ready"), times(g - 1))
                            for k in range(2):
                                sp.dma_start(region[k][par][:], slot_rows[:, bass.ds(g * GS + k * NSL, GS), :])\
                                  .then_inc(sem(f"region_in{par}"), 16)
                            if j % GPE == 0 and at_least(e, 1) and exists(e + 1):
                                sp.wait_ge(sem("w1_split"), e)
                                sp.dma_start(w1_nat[1 - w][:], w1_rows[bass.ds((e + 1) * P, P), :]).then_inc(sem(f"w1_in{1 - w}"), 16)
                        on_groups(sp, step)

                    @block.gpsimd
                    def _(pool):
                        def scatter(g, j, par):
                            pool.wait_ge(sem("y_out"), g + 1)
                            apart(pool)
                            for t in range(GS):
                                pool.indirect_dma_start(
                                    out=y_rows[:, :], out_offset=bass.IndirectOffsetOnAxis(ap=row_id[j][:, t:t + 1].bitcast(U32), axis=0),
                                    in_=y_sb[par][:, t, :], in_offset=None, bounds_check=2 * N - 1, oob_is_err=False,
                                ).then_inc(sem(f"y_stored{par}"), 16)
                        pool.wait_ge(sem("y_zeroed"), 16 * (2 * N // (P * BLANK)))
                        on_groups(pool, lambda g, j, e: scatter(g, j, j % 2))
                        for par in range(2):
                            pool.wait_ge(sem(f"y_stored{par}"), NG // 2 * 16 * GS)

                    @block.tensor
                    def _(pe):
                        def down(g, par, w):
                            pe.wait_ge(sem(f"w2_in{w}"), times(((g >> 2) + 1) * 16))
                            pe.wait_ge(sem("hid3_out"), g + 1)
                            pe.wait_ge(sem("y_out"), times(g - 1))
                            for t in range(GS):
                                for k in range(KH):
                                    mm = pe.matmul(psum[6 + par][:, t * D:(t + 1) * D], hidden[par][:, k, t * P:(t + 1) * P],
                                                   w2_sb[w][:, k, :], start=(k == 0), stop=(k == KH - 1))
                            mm.then_inc(sem("y_in"), 1)

                        def step(g, j, e):
                            par, w = j % 2, j // GPE
                            pe.wait_ge(sem("rows_ready"), g + 1)
                            pe.wait_ge(sem("rowsT_split"), times(g - 1))
                            for t in range(GS):
                                mm = pe.transpose(psum[par][:, t * P:(t + 1) * P], rows[par][:, t, 0:D], ident[:])
                            mm.then_inc(sem("rowsT_in"), 1)
                            if at_least(g, 2):
                                down(g - 2, par, 1 - w)
                            pe.wait_ge(sem("rowsT_split"), g + 1)
                            pe.wait_ge(sem("w1_split"), e + 1)
                            for k in range(KH):
                                pe.wait_ge(sem(f"hid{k}_out"), g)
                                o, ks = psum[2 + k][:], slice(k * P, (k + 1) * P)
                                pe.matmul(o, w1_hi[w][:, ks], rowsT_hi[par][:], start=True, stop=False)
                                pe.matmul(o, w1_lo[w][:, ks], rowsT_hi[par][:], start=False, stop=False)
                                pe.matmul(o, w1_hi[w][:, ks], rowsT_lo[par][:], start=False, stop=True).then_inc(sem(f"hid{k}_in"), 1)
                        on_groups(pe, step)
                        down(NG - 2, 0, 1)
                        down(NG - 1, 1, 1)

                    @block.scalar
                    def _(act):
                        act.wait_ge(sem("shifted"), 1)
                        act.activation(prob[:], shifted[:], ACT.Exp).then_inc(sem("prob_exp"), 1)

                        def step(g, j, e):
                            par = j % 2
                            act.wait_ge(sem("rowsT_in"), g + 1)
                            act.wait_ge(sem("hid3_in"), times(g - 1))
                            act.copy(rowsT_hi[par][:], psum[par][:]).then_inc(sem("rowsT_hi_done"), 1)
                            act.wait_ge(sem("y_in"), times(g - 1))
                            for k in range(KH):
                                act.wait_ge(sem(f"hid{k}_in"), g + 1)
                                apart(act)
                                act.activation(hidden[par][:, k, :], psum[2 + k][:], ACT.Gelu,
                                               bias=b1_col[:, bass.ds(e * KH + k, 1)]).then_inc(sem(f"hid{k}_out"), 1)
                            if j % GPE == 1 and at_least(e, 1) and exists(e + 1):
                                w = j // GPE
                                act.wait_ge(sem("y_in"), g - 1)
                                act.dma_start(w2_sb[1 - w][:], w2_rows[:, bass.ds((e + 1) * KH, KH), :]).then_inc(sem(f"w2_in{1 - w}"), 16)
                        on_groups(act, step)

                    @block.vector
                    def _(dve):
                        def split_w1(e, w, g):
                            dve.wait_ge(sem(f"w1_in{w}"), ((e >> 1) + 1) * 16)
                            dve.wait_ge(sem("hid3_in"), times(g))
                            dve.tensor_copy(w1_hi[w][:], w1_nat[w][:]).then_inc(sem("w1_hi_done"), 1)
                            dve.wait_ge(sem("w1_hi_done"), e + 1)
                            dve.tensor_tensor(w1_lo[w][:], w1_nat[w][:], w1_hi[w][:].bitcast(F32), ALU.subtract).then_inc(sem("w1_split"), 1)

                        def merge(g, j, par):
                            dve.wait_ge(sem(f"region_in{par}"), ((g >> 1) + 1) * 32)
                            dve.wait_ge(sem("rowsT_in"), times(g - 1))
                            apart(dve)
                            for t in range(GS):
                                ins = dve.scalar_tensor_tensor(out=rows[par][:, t, :], in0=region[1][par][:, t, :],
                                                               scalar=second[:, bass.ds(g * GS + t, 1)],
                                                               in1=region[0][par][:, t, :], op0=ALU.mult, op1=ALU.add)
                            ins.then_inc(sem("rows_ready"), 1)
                            dve.wait_ge(sem("rows_ready"), g + 1)
                            if at_least(g, 4):
                                dve.wait_ge(sem(f"y_stored{par}"), ((g - 2) >> 1) * 16 * GS)
                            apart(dve)
                            dve.scalar_tensor_tensor(out=row_id[j][:], in0=second[:, bass.ds(g * GS, GS)], scalar=float(N),
                                                     in1=rows[par][:, :, D], op0=ALU.mult, op1=ALU.add).then_inc(sem("ids_ready"), 1)

                        def y_out(g, par, e):
                            dve.wait_ge(sem("y_in"), g + 1)
                            dve.wait_ge(sem(f"y_stored{par}"), times((g >> 1) * 16 * GS))
                            dve.tensor_tensor(y_sb[par][:], psum[6 + par][:].rearrange("p (t d) -> p t d", d=D),
                                              b2_b[:, bass.ds(e * D, D)].unsqueeze(1).to_broadcast([P, GS, D]), ALU.add)\
                               .then_inc(sem("y_out"), 1)

                        n = [0]

                        def link(ins):
                            n[0] += 1
                            ins.then_inc(sem("weight_step"), 1)
                            dve.wait_ge(sem("weight_step"), n[0])

                        def softmax_weights():
                            dve.wait_ge(sem("prob_exp"), 1)
                            link(dve.tensor_reduce(total[:], prob[:], AX, ALU.add))
                            link(dve.reciprocal(total[:], total[:]))
                            link(dve.tensor_tensor(weight[:], prob[:, :, 0:2], total[:].unsqueeze(2).to_broadcast([P, NCH, 2]), ALU.mult))
                            link(dve.tensor_reduce(total[:], weight[:], AX, ALU.add))
                            link(dve.tensor_scalar(total[:], total[:], 1e-9, None, ALU.max))
                            link(dve.reciprocal(total[:], total[:]))
                            link(dve.tensor_tensor(weight[:], weight[:], total[:].unsqueeze(2).to_broadcast([P, NCH, 2]), ALU.mult))

                        link(dve.tensor_tensor(second[:].rearrange("p (e t) -> p e t", t=TPE),
                                               slot_number[:].rearrange("p (e t) -> p e t", t=TPE),
                                               taken[:, 0:E].unsqueeze(2).to_broadcast([P, E, TPE]), ALU.is_gt))
                        tops = top_logits[:].rearrange("p (c e) -> p c e", e=E)
                        dve.tensor_tensor(shifted[:], tops, tops[:, :, 0:1].to_broadcast([P, NCH, E]), ALU.subtract).then_inc(sem("shifted"), 1)

                        def step(g, j, e):
                            par, w = j % 2, j // GPE
                            merge(g, j, par)
                            dve.wait_ge(sem("rowsT_hi_done"), g + 1)
                            dve.tensor_tensor(rowsT_lo[par][:], psum[par][:], rowsT_hi[par][:].bitcast(F32), ALU.subtract).then_inc(sem("rowsT_split"), 1)
                            if j % GPE == 1 and exists(e + 1):
                                split_w1(e + 1, 1 - w, g - 1)
                            if isinstance(g, int) and g == 0:
                                softmax_weights()
                            if at_least(g, 2):
                                y_out(g - 2, par, e - 1)
                        split_w1(0, 0, 0)
                        on_groups(dve, step)
                        y_out(NG - 2, 0, E - 1)
                        y_out(NG - 1, 1, E - 1)
        experts()

        def combine():
            with ExitStack() as tmp:
                def tsb(name, shape, dt=F32):
                    return tmp.enter_context(nc.sbuf_tensor(name, shape, dt))
                y = [[tsb(f"y{k}_{b}", [P, CPB, D]) for b in range(B)] for k in range(2)]
                y_v = y_rows.rearrange("(a p) d -> p a d", p=P)
                with nc.Block() as block:
                    @block.sync
                    def _(sp):
                        for b in range(B):
                            for k in range(2):
                                sp.dma_start(y[k][b][:], y_v[:, k * NCH + b * CPB:k * NCH + (b + 1) * CPB, :])\
                                  .then_inc(sem(f"y_loaded{b}"), 16)
                        for b in range(B):
                            sp.wait_ge(sem("out_ready"), b + 1)
                            sp.dma_start(out_v[:, b * CPB:(b + 1) * CPB, :],
                                         x_sb[:, b * CPB * D:(b + 1) * CPB * D].rearrange("p (c d) -> p c d", d=D)).then_inc(sem("out_stored"), 16)
                        sp.wait_ge(sem("out_stored"), 16 * B)

                    @block.scalar
                    def _(act):
                        for b in range(B):
                            act.wait_ge(sem(f"y_loaded{b}"), 32)
                            for i in range(CPB):
                                t = y[0][b][:, i, :]
                                ins = act.activation(t, t, ACT.Copy, scale=weight[:, b * CPB + i, 0:1])
                            ins.then_inc(sem("scaled"), 1)

                    @block.vector
                    def _(dve):
                        for b in range(B):
                            dve.wait_ge(sem("scaled"), b + 1)
                            for i in range(CPB):
                                t = y[1][b][:, i, :]
                                ins = dve.scalar_tensor_tensor(out=t, in0=t, scalar=weight[:, b * CPB + i, 1:2], in1=y[0][b][:, i, :],
                                                               op0=ALU.mult, op1=ALU.add)
                            ins.then_inc(sem("combine_step"), 1)
                            dve.wait_ge(sem("combine_step"), 2 * b + 1)
                            dve.tensor_tensor(y[1][b][:], y[1][b][:], gb_b[:, b * D:(b + 1) * D].unsqueeze(1).to_broadcast([P, CPB, D]),
                                              ALU.mult).then_inc(sem("combine_step"), 1)

                    @block.gpsimd
                    def _(pool):
                        for b in range(B):
                            xs = x_sb[:, b * CPB * D:(b + 1) * CPB * D].rearrange("p (c d) -> p c d", d=D)
                            pool.wait_ge(sem("combine_step"), 2 * b + 2)
                            pool.tensor_tensor(xs, xs, y[1][b][:], ALU.add).then_inc(sem("out_ready"), 1)
        combine()


_INS = ["L0_attn_x", "L0_attn_omega", "L0_attn_wq", "L0_attn_wk", "L0_attn_wv", "L0_attn_wo", "L0_attn_bo",
        "L0_ffn_wg", "L0_ffn_w1", "L0_ffn_b1", "L0_ffn_w2", "L0_ffn_b2", "L0_c", "L0_wmod"]
_OUTS = [((4, 1024, 128), "float32")]


def kernel(**inputs):
    import numpy as _np
    import concourse.bacc as _bacc
    from concourse import mybir as _mybir
    from concourse.bass_utils import run_bass_kernel_spmd as _run

    nc = _bacc.Bacc("TRN2", target_bir_lowering=False, num_devices=1)
    arrays, args = {}, []
    for name in _INS:
        a = _np.ascontiguousarray(inputs[name])
        arrays[f"in_{name}_dram"] = a
        args.append(nc.dram_tensor(f"in_{name}_dram", a.shape, _mybir.dt.from_np(a.dtype), kind="ExternalInput").ap())
    for i, (shape, dtype) in enumerate(_OUTS):
        dt = _mybir.dt.from_np(_np.dtype(dtype))
        args.append(nc.dram_tensor(f"out_{i}_dram", shape, dt, kind="ExternalOutput").ap())
    build(nc, *args)
    r = _run(nc, [arrays], core_ids=[0])
    got = tuple(r.results[0][f"out_{i}_dram"] for i in range(len(_OUTS)))
    return got[0]
```

```python
from contextlib import ExitStack

import concourse.bass as bass
from concourse import mybir

F32 = mybir.dt.float32
F32R = mybir.dt.float32r
BF16 = mybir.dt.bfloat16
I32 = mybir.dt.int32
U32 = mybir.dt.uint32
ALU = mybir.AluOpType
ACT = mybir.ActivationFunctionType
AX = mybir.AxisListType.X

P = 128


def build(nc, x, omega, wq, wk, wv, wo, bo, wg, w1, b1, w2, b2, cond, wmod, out):
    B, S, D = x.shape
    M, DH = omega.shape
    HD = wq.shape[0]
    H = HD // DH
    NP = H // 2
    E, _, HID = w1.shape
    KH = HID // P
    N = B * S
    NCH = N // P
    CPB = S // P
    SHIFT = CPB.bit_length() - 1
    CAP = (2 * N + E - 1) // E
    NSL = E * CAP // P
    TPE = CAP // P
    GS = 4
    NG = NSL // GS
    RW = D + 3
    BLANK = 8
    VW = DH + 1
    PW = 2 * VW
    SKIP = 200000
    FEATURE_SCALE = float(M) ** -0.5
    assert D == P and DH == 64 and M == 64 and E == 8 and CAP % (GS * P) == 0 and HD == 1024

    dispatched = nc.dram_tensor("dispatched", [2 * E * CAP, RW], F32, kind="Internal").ap()
    y_rows = nc.dram_tensor("y_rows", [2 * N, D], F32, kind="Internal").ap()

    with ExitStack() as ctx:
        def sb(name, shape, dt=F32):
            return ctx.enter_context(nc.sbuf_tensor(name, shape, dt))

        sems = {}

        def sem(name):
            if name not in sems:
                sems[name] = ctx.enter_context(nc.semaphore(name))
            return sems[name]

        def times(count, most=None):
            if not isinstance(count, int):
                return count
            return max(count, 0) if most is None else min(max(count, 0), most)

        def apart(eng):
            eng.sem_inc(sem("wait_passed"), 1)

        x_sb = sb("x_sb", [P, NCH * D])
        wT_hi = {k: sb(f"w{k}_hi", [P, HD], F32R) for k in ("q", "k", "v", "pq", "pk")}
        wT_lo = {k: sb(f"w{k}_lo", [P, HD], F32R) for k in ("q", "k", "v", "pq", "pk")}
        woT = sb("woT", [P, NP, D])
        wg_sb = sb("wg_sb", [P, E])
        ident = sb("ident", [P, P])
        causal = sb("causal", [P, 4, P])
        keep = sb("keep", [P, NCH], U32)
        sa_col = sb("sa_col", [P, B + 1])
        ca_col = sb("ca_col", [P, B + 1])
        ga_b = sb("ga_b", [P, (B + 1) * D])
        sb_b = sb("sb_b", [P, (B + 1) * D])
        cb_b = sb("cb_b", [P, (B + 1) * D])
        gb_b = sb("gb_b", [P, (B + 1) * D])
        bo_b = sb("bo_b", [P, D])
        b2_b = sb("b2_b", [P, E * D])
        b1_col = sb("b1_col", [P, E * KH])
        token = sb("token", [P, NCH])
        iota_e = sb("iota_e", [P, E])
        first_limit = sb("first_limit", [P, E])
        second_limit = sb("second_limit", [P, E])
        taken = sb("taken", [P, 2 * E])
        sign = sb("sign", [P, 2])
        slot_number = sb("slot_number", [P, NSL])
        tri = sb("tri", [P, P], BF16)
        ones = sb("ones", [P, P], BF16)
        blank = [sb(f"blank{i}", [P, BLANK, RW]) for i in range(2)]
        w1_nat = [sb(f"w1_nat{i}", [P, HID]) for i in range(2)]
        w2_sb = [sb(f"w2_sb{i}", [P, KH, D]) for i in range(2)]
        w1_rows = w1.rearrange("e d h -> (e d) h")
        w2_rows = w2.rearrange("e (k p) d -> p (e k) d", p=P)

        psum = [ctx.enter_context(nc.psum_tensor(f"bank{i}", [P, 512], F32)) for i in range(8)]

        x_v = x.rearrange("b (c p) d -> p (b c) d", p=P)
        out_v = out.rearrange("b (c p) d -> p (b c) d", p=P)

        xn = [sb(f"xn{i}", [P, D]) for i in range(2)]
        st1 = sb("st1", [P, 6])
        mv1 = sb("mv1", [P, 2])
        rs1 = sb("rs1", [P, 1])
        var1 = sb("var1", [P, 1])
        power = sb("power", [P, 1])

        def moments(dve, tag, src, st, mv, var, n):
            apart(dve)
            dve.bn_stats(st[:], src).then_inc(sem(tag + "_step"), 1)
            dve.wait_ge(sem(tag + "_step"), 2 * n - 1)
            apart(dve)
            dve.bn_aggr(mv[:], st[:]).then_inc(sem(tag + "_step"), 1)
            dve.wait_ge(sem(tag + "_step"), 2 * n)
            dve.tensor_scalar(var[:], mv[:, 1:2], 1e-5, None, ALU.add).then_inc(sem(tag + "_var"), 1)

        def rstd(pool, tag, var, rs, n):
            pool.wait_ge(sem(tag + "_var"), n)
            pool.tensor_tensor(rs[:], var[:], power[:], ALU.pow).then_inc(sem(tag + "_rstd"), 1)

        def first_moments(dve, n):
            dve.wait_ge(sem("xn_ready"), n)
            moments(dve, "ln1", x_sb[:, bass.ds(n * D, D)], st1, mv1, var1, n + 1)

        def first_norm(dve, n, par):
            dve.wait_ge(sem("hT_in"), times(n - 1))
            dve.wait_ge(sem("ln1_rstd"), n + 1)
            dve.tensor_scalar(xn[par][:], x_sb[:, bass.ds(n * D, D)], mv1[:, 0:1], rs1[:, 0:1],
                              ALU.subtract, ALU.mult).then_inc(sem("xn_ready"), 1)

        def setup():
            with ExitStack() as tmp:
                def tsb(name, shape, dt=F32):
                    return tmp.enter_context(nc.sbuf_tensor(name, shape, dt))
                w_nat = {k: tsb(f"w{k}_nat", [P, NP, D]) for k in ("q", "k", "v")}
                wo_nat = tsb("wo_nat", [P, HD])
                om_blk = tsb("om_blk", [P, P])
                omT_blk = tsb("omT_blk", [P, P])
                c_nat = tsb("c_nat", [B, D])
                c_sig = tsb("c_sig", [B, D])
                c_silu = tsb("c_silu", [B, D])
                siluT = tsb("siluT", [P, B])
                silu_b = tsb("silu_b", [P, B, P])
                wmod_sb = tsb("wmod_sb", [P, 6 * D])
                b1_nat = tsb("b1_nat", [E * KH, P])
                with nc.Block() as block:
                    @block.sync
                    def _(sp):
                        sp.dma_start(w_nat["q"][:], wq.rearrange("(j p) d -> p j d", p=P)).then_inc(sem("wq_loaded"), 16)
                        sp.wait_ge(sem("om_zeroed"), 1)
                        for i in range(2):
                            sp.dma_start(om_blk[i * M:(i + 1) * M, i * DH:(i + 1) * DH], omega).then_inc(sem("s_om"), 16)
                        for k, w in (("k", wk), ("v", wv)):
                            sp.dma_start(w_nat[k][:], w.rearrange("(j p) d -> p j d", p=P)).then_inc(sem("kv_loaded"), 16)
                        for i in range(4):
                            n = NCH // 4
                            sp.dma_start(x_sb[:, i * n * D:(i + 1) * n * D].rearrange("p (c d) -> p c d", d=D),
                                         x_v[:, i * n:(i + 1) * n, :]).then_inc(sem("later_loads" if i else "x_begun"), 16)
                            if i == 0:
                                sp.dma_start(wo_nat[:], wo).then_inc(sem("wo_loaded"), 16)
                                sp.dma_start(b1_nat[:], b1.rearrange("e (k p) -> (e k) p", p=P)).then_inc(sem("s_b1"), 16)
                        sp.wait_ge(sem("blank_ready"), 1)
                        for region in range(2):
                            for i in range(E * CAP // (P * BLANK)):
                                r0 = region * E * CAP + i * P * BLANK
                                sp.dma_start(dispatched[r0:r0 + P * BLANK, :].rearrange("(p r) d -> p (r d)", p=P),
                                             blank[region][:].rearrange("p r d -> p (r d)")).then_inc(sem("dispatched_blank"), 16)
                        for i in range(2 * N // (P * BLANK)):
                            sp.dma_start(y_rows[i * P * BLANK:(i + 1) * P * BLANK, :].rearrange("(p r) d -> p (r d)", p=P),
                                         blank[0][:].rearrange("p r d -> p (r d)")[:, 0:BLANK * D]).then_inc(sem("y_zeroed"), 16)

                    @block.scalar
                    def _(act):
                        act.dma_start(c_nat[:], cond).then_inc(sem("s_c"), 16)
                        act.dma_start(wmod_sb[:], wmod).then_inc(sem("s_wmod"), 16)
                        act.dma_start(wg_sb[:], wg).then_inc(sem("later_loads"), 16)
                        act.dma_start(bo_b[:], bo.rearrange("(a d) -> a d", a=1).to_broadcast([P, D])).then_inc(sem("later_loads"), 16)
                        act.dma_start(b2_b[:], b2.rearrange("(a e) d -> a (e d)", a=1).to_broadcast([P, E * D])).then_inc(sem("later_loads"), 16)
                        act.wait_ge(sem("s_c"), 16)
                        nc.scalar.activation(c_sig[:], c_nat[:], ACT.Exp, scale=-1.0).then_inc(sem("c_exp"), 1)
                        for n, (k, half) in enumerate(WEIGHTS):
                            act.wait_ge(sem("wT_filled"), n + 1)
                            nc.scalar.copy(wT_hi[k][:, half * 512:(half + 1) * 512], psum[n % 4][:]).then_inc(sem("wT_hi_done"), 1)

                    @block.gpsimd
                    def _(pool):
                        nc.gpsimd.memset(om_blk[:], 0.0).then_inc(sem("om_zeroed"), 1)
                        nc.gpsimd.memset(ident[:], 0.0).then_inc(sem("p_chain"), 1)
                        nc.gpsimd.memset(causal[:], 1.0).then_inc(sem("p_chain"), 1)
                        pool.wait_ge(sem("p_chain"), 2)
                        nc.gpsimd.affine_select(out=ident[:], in_=ident[:], compare_op=ALU.not_equal, fill=1.0, base=0,
                                                pattern=[[-1, P]], channel_multiplier=1).then_inc(sem("ident_ready"), 1)
                        nc.gpsimd.affine_select(out=causal[:], in_=causal[:], compare_op=ALU.is_ge, fill=0.0, base=0,
                                                pattern=[[0, 4], [1, P]], channel_multiplier=-1).then_inc(sem("p_chain"), 1)
                        for i in range(2):
                            nc.gpsimd.memset(blank[i][:], 0.0).then_inc(sem("p_chain"), 1)
                        pool.wait_ge(sem("p_chain"), 5)
                        nc.gpsimd.memset(blank[1][:, :, D:D + 1], float(SKIP)).then_inc(sem("blank_ready"), 1)
                        nc.gpsimd.tensor_copy(tri[:], causal[:, 0, :]).then_inc(sem("tables"), 1)
                        nc.gpsimd.memset(ones[:], 1.0).then_inc(sem("tables"), 1)
                        nc.gpsimd.memset(sign[:, 0:1], 1.0).then_inc(sem("tables"), 1)
                        nc.gpsimd.memset(sign[:, 1:2], -1.0).then_inc(sem("tables"), 1)

                        def iota(t, step, base, mult=0):
                            nc.gpsimd.iota(t, pattern=[[step, t.shape[1]]], base=base, channel_multiplier=mult,
                                           allow_small_or_imprecise_dtypes=True).then_inc(sem("tables"), 1)
                        iota(token[:], P, 0, 1)
                        iota(slot_number[:], P, 0, 1)
                        iota(iota_e[:], 1, 0)
                        iota(first_limit[:], CAP, CAP - 1)
                        iota(second_limit[:], CAP, E * CAP)
                        iota(taken[:, 0:E], CAP, -1)
                        iota(taken[:, E:2 * E], CAP, (E + 1) * CAP)
                        pool.wait_ge(sem("tables"), 11)
                        nc.gpsimd.memset(power[:], -0.5).then_inc(sem("power_set"), 1)
                        pool.wait_ge(sem("power_set"), 1)
                        rstd(pool, "ln1", var1, rs1, 1)

                    @block.tensor
                    def _(pe):
                        pe.wait_ge(sem("ident_ready"), 1)
                        pe.wait_ge(sem("silu_ready"), 1)
                        pe.transpose(psum[7][:, 0:B], c_silu[:], ident[0:B, 0:B]).then_inc(sem("small_filled"), 1)
                        pe.wait_ge(sem("s_om"), 32)
                        pe.transpose(psum[6][:, 0:P], om_blk[:], ident[:]).then_inc(sem("small_filled"), 1)
                        pe.wait_ge(sem("s_wmod"), 16)
                        pe.wait_ge(sem("small_used"), 1)
                        pe.matmul(psum[7][:, 0:B], wmod_sb[:, 0:D], siluT[:], start=True, stop=True)
                        pe.matmul(psum[7][:, 64:64 + B], wmod_sb[:, D:2 * D], siluT[:], start=True, stop=True).then_inc(sem("mod_filled"), 1)

                        def modulation(m, bank):
                            for b in range(B):
                                mm = pe.matmul(psum[bank][:, b * D:(b + 1) * D], silu_b[:, b, :],
                                               wmod_sb[:, (2 + m) * D:(3 + m) * D], start=True, stop=True)
                            mm.then_inc(sem("mod_filled"), 1)

                        def weights(n, k, half):
                            if n >= 4:
                                pe.wait_ge(sem("wT_split"), n - 3)
                            dst = psum[n % 4]
                            src = w_nat[k[-1]]
                            for j in range(4):
                                t = half * 4 + j
                                o = dst[:, j * P:(j + 1) * P]
                                if k in "qkv":
                                    mm = pe.transpose(o, src[:, t, :], ident[:])
                                else:
                                    mm = pe.matmul(o, src[:, t, :], omT_blk[:], start=True, stop=True)
                            mm.then_inc(sem("wT_filled"), 1)
                        pe.wait_ge(sem("wq_loaded"), 16)
                        pe.wait_ge(sem("small_used"), 2)
                        for n, (k, half) in enumerate(WEIGHTS):
                            if n == 4:
                                pe.wait_ge(sem("kv_loaded"), 32)
                            weights(n, k, half)
                            if n >= 4 and n < 8:
                                if n == 7:
                                    pe.wait_ge(sem("mod_used"), 1)
                                modulation(n - 4, 4 + (n - 4) % 3)
                        pe.wait_ge(sem("s_b1"), 16)
                        pe.wait_ge(sem("small_used"), 3)
                        pe.transpose(psum[7][:, 0:E * KH], b1_nat[:], ident[0:E * KH, 0:E * KH]).then_inc(sem("small_filled"), 1)
                        pe.wait_ge(sem("wo_loaded"), 16)
                        for half in range(2):
                            pe.wait_ge(sem("mod_used"), 2 + half)
                            for j in range(4):
                                t = half * 4 + j
                                mm = pe.transpose(psum[5 + half][:, j * P:(j + 1) * P], wo_nat[:, t * P:(t + 1) * P], ident[:])
                            mm.then_inc(sem("woT_filled"), 1)

                    @block.vector
                    def _(dve):
                        dve_n = [0]

                        def link(ins):
                            dve_n[0] += 1
                            ins.then_inc(sem("d_chain"), 1)
                            dve.wait_ge(sem("d_chain"), dve_n[0])
                        link(dve.memset(keep[:], 0xFFFFFFFF))
                        link(dve.memset(keep[:].rearrange("p (b c) -> p b c", c=CPB)[:, :, 0:1], 0))
                        dve.wait_ge(sem("c_exp"), 1)
                        link(dve.tensor_scalar(c_sig[:], c_sig[:], 1.0, None, ALU.add))
                        link(dve.reciprocal(c_sig[:], c_sig[:]))
                        dve.tensor_tensor(c_silu[:], c_nat[:], c_sig[:], ALU.mult).then_inc(sem("silu_ready"), 1)
                        dve.wait_ge(sem("small_filled"), 1)
                        link(dve.tensor_copy(siluT[:], psum[7][:, 0:B]))
                        dve.tensor_copy(silu_b[:], siluT[:].unsqueeze(2).to_broadcast([P, B, P])).then_inc(sem("small_used"), 1)
                        dve.wait_ge(sem("small_filled"), 2)
                        dve.tensor_copy(omT_blk[:], psum[6][:, 0:P]).then_inc(sem("small_used"), 1)
                        dve.wait_ge(sem("mod_filled"), 1)
                        link(dve.tensor_copy(sa_col[:, 0:B], psum[7][:, 0:B]))
                        dve.tensor_scalar(ca_col[:, 0:B], psum[7][:, 64:64 + B], 1.0, None, ALU.add).then_inc(sem("small_used"), 1)
                        for n, (k, half) in enumerate(WEIGHTS):
                            dve.wait_ge(sem("wT_hi_done"), n + 1)
                            cols = slice(half * 512, (half + 1) * 512)
                            dve.tensor_tensor(wT_lo[k][:, cols], psum[n % 4][:], wT_hi[k][:, cols].bitcast(F32),
                                              ALU.subtract).then_inc(sem("wT_split"), 1)
                            if n == 3:
                                dve.wait_ge(sem("x_begun"), 16)
                                first_moments(dve, 0)
                            if n == 4:
                                first_norm(dve, 0, 0)
                            if n >= 5 and n < 9:
                                m = n - 5
                                t = (ga_b, sb_b, cb_b, gb_b)[m]
                                dve.wait_ge(sem("mod_filled"), m + 2)
                                if t is cb_b:
                                    dve.tensor_scalar(t[:, 0:B * D], psum[4 + m % 3][:], 1.0, None, ALU.add).then_inc(sem("mod_used"), 1)
                                else:
                                    dve.tensor_copy(t[:, 0:B * D], psum[4 + m % 3][:]).then_inc(sem("mod_used"), 1)
                        dve.wait_ge(sem("small_filled"), 3)
                        dve.tensor_copy(b1_col[:], psum[7][:, 0:E * KH]).then_inc(sem("small_used"), 1)
                        for half in range(2):
                            dve.wait_ge(sem("woT_filled"), half + 1)
                            link(dve.tensor_copy(woT[:, half * 4:half * 4 + 4, :].rearrange("p j d -> p (j d)"), psum[5 + half][:]))
                        dve.wait_ge(sem("wT_split"), len(WEIGHTS))

        WEIGHTS = [(k, half) for k in ("q", "pq", "k", "v", "pk") for half in range(2)]
        setup()

        def attention():
            with ExitStack() as tmp:
                def tsb(name, shape, dt=F32):
                    return tmp.enter_context(nc.sbuf_tensor(name, shape, dt))
                var2 = tsb("var2", [P, 1])
                h_full = tsb("h_full", [P, P])
                h_hi = [tsb(f"h_hi{i}", [P, P], F32R) for i in range(2)]
                h_lo = [tsb(f"h_lo{i}", [P, P], F32R) for i in range(2)]
                square = {k: tsb(f"square_{k}", [P, HD]) for k in "qk"}
                norm = {k: tsb(f"norm_{k}", [P, H]) for k in "qk"}
                expo = {k: tsb(f"expo_{k}", [P, HD]) for k in "qk"}
                phi = {k: [tsb(f"phi_{k}{i}", [P, HD]) for i in range(2)] for k in "qk"}
                phiT = {k: tsb(f"phiT_{k}", [P, NP, P]) for k in "qk"}
                v_sb = [tsb(f"v_sb{i}", [P, H, VW]) for i in range(2)]
                scores = tsb("scores", [P, H, P])
                state = [tsb(f"state{i}", [P, NP, PW]) for i in range(2)]
                den = [tsb(f"den{i}", [P, 4]) for i in range(2)]
                rden = [tsb(f"rden{i}", [P, 4]) for i in range(2)]
                att = tsb("att", [P, H, DH])
                attT = tsb("attT", [P, NP, P])
                upd = [tsb(f"upd{i}", [P, D]) for i in range(2)]
                st2 = tsb("st2", [P, 6])
                mv2 = tsb("mv2", [P, 2])
                rs2 = tsb("rs2", [P, 1])
                x2_now = tsb("x2_now", [P, D])
                xn2 = tsb("xn2", [P, D])
                xm2 = tsb("xm2", [P, D])
                h2T = tsb("h2T", [P, P])
                sgn = tsb("sgn", [P, B * D])
                mag = tsb("mag", [P, B * D])
                lg_now = tsb("lg_now", [P, E])
                top = tsb("top", [P, E])
                below = tsb("below", [P, E])
                prob = tsb("prob", [P, E])
                total = tsb("total", [P, 1])
                pair = tsb("pair", [P, 2])
                best = tsb("best", [P, E], U32)
                best_f = tsb("best_f", [P, 2])
                hot = tsb("hot", [P, 2 * E], BF16)
                place = tsb("place", [P, 2 * E])
                over = tsb("over", [P, 2 * E])
                slot_f = tsb("slot_f", [P, 2])
                slot = [tsb(f"slot{i}", [P, 2], I32) for i in range(2)]

                TURNS = {0: ["q0", "k0", "pq0", "pk0", "v0"], 1: ["q1", "k1", "pq1", "pk1", "v1"],
                         2: ["tk0", "tk1", "a0", "a2"], 3: ["tq0", "tq1", "a1", "a3"],
                         4: ["attT0", "o0", "o2"], 5: ["attT1", "o1", "o3"],
                         6: ["kv0", "kv1", "kv2"], 7: ["h2T", "lg", "rank", "wo", "hT"]}
                BANK = {k: b for b, ks in TURNS.items() for k in ks}
                BEFORE = {k: ks[i - 1] for ks in TURNS.values() for i, k in enumerate(ks)}

                def on_steps(eng, step):
                    for c in range(-2, 4):
                        step(c, c % 2)
                    with eng.Fori(2, NCH // 2 - 2) as i:
                        for j in range(2):
                            step(2 * i + j, j)
                    for c in range(NCH - 4, NCH + 2):
                        step(c, c % 2)

                def live(c, ahead=0):
                    return not isinstance(c, int) or 0 <= c + ahead < NCH

                with nc.Block() as block:
                    @block.tensor
                    def _(pe):
                        def project(kind, c, par):
                            if kind[:-1] == "q":
                                pe.wait_ge(sem(f"v{kind[-1]}_out"), times(c + 1))
                            else:
                                pe.wait_ge(sem(BEFORE[kind] + "_out"), c + 2)
                            o = psum[BANK[kind]][:]
                            w, half = kind[:-1], int(kind[-1])
                            cols = slice(half * 512, (half + 1) * 512)
                            pe.matmul(o, h_hi[par][:], wT_hi[w][:, cols], start=True, stop=False)
                            pe.matmul(o, h_hi[par][:], wT_lo[w][:, cols], start=False, stop=False)
                            pe.matmul(o, h_lo[par][:], wT_hi[w][:, cols], start=False, stop=True).then_inc(sem(kind + "_in"), 1)

                        def features_T(kind, c, par):
                            k, half = kind[1], int(kind[2])
                            if half:
                                pe.wait_ge(sem(f"t{k}0_out"), c + 1)
                            else:
                                pe.wait_ge(sem("a2_out" if k == "k" else "a3_out"), c)
                            pe.wait_ge(sem(f"phi_{k}_ready"), c + 1)
                            for j in range(4):
                                t = half * 4 + j
                                mm = pe.transpose(psum[BANK[kind]][:, j * P:(j + 1) * P], phi[k][par][:, t * P:(t + 1) * P], ident[:])
                            mm.then_inc(sem(kind + "_in"), 1)

                        def score(half, c):
                            for z in range(2):
                                pe.wait_ge(sem(f"a{z}_out" if half else f"t{'kq'[z]}1_out"), c + 1)
                            pe.wait_ge(sem(f"tk{half}_out"), c + 1)
                            pe.wait_ge(sem(f"tq{half}_out"), c + 1)
                            for j in range(4):
                                for z in range(2):
                                    r, kind = slice(z * M, (z + 1) * M), f"a{2 * half + z}"
                                    mm = pe.matmul(psum[BANK[kind]][:, j * P:(j + 1) * P], phiT["k"][r, half * 4 + j, :],
                                                   phiT["q"][r, half * 4 + j, :], start=True, stop=True)
                                    if j == 3:
                                        mm.then_inc(sem(kind + "_in"), 1)

                        def attend(g, c, par):
                            kind = f"o{g}"
                            if g < 2:
                                pe.wait_ge(sem(f"attT{g}_out"), c)
                            else:
                                pe.wait_ge(sem(f"o{g - 2}_out"), c + 1)
                            pe.wait_ge(sem("state_kept" if par == 0 else "kv2_out"), times(c + 1 - par))
                            for z in range(2):
                                pe.wait_ge(sem(f"a{g // 2 * 2 + z}_out"), c + 1)
                            for q in range(2):
                                p = g * 2 + q
                                pe.matmul(psum[BANK[kind]][:, q * PW:(q + 1) * PW], phiT["q"][:, p, :], state[par][:, p, :],
                                          start=(q == 0), stop=False, skip_group_check=True)
                                for z in range(2):
                                    h = 2 * p + z
                                    mm = pe.matmul(psum[BANK[kind]][:, q * PW + z * VW:q * PW + (z + 1) * VW],
                                                   scores[:, (p // 4 * 2 + z) * 4 + p % 4, :], v_sb[par][:, h, :], start=False,
                                                   stop=(q == 1 and z == 1), skip_group_check=True)
                            mm.then_inc(sem(kind + "_in"), 1)

                        def state_gain(g, c, par):
                            kind = f"kv{g}"
                            pe.wait_ge(sem(f"kv{(g - 1) % 3}_out"), c + min(g, 1))
                            for q, p in enumerate(KV_PAIRS[g]):
                                mm = pe.matmul(psum[BANK[kind]][:, q * PW:(q + 1) * PW], phi["k"][par][:, p * P:(p + 1) * P],
                                               v_sb[par][:, 2 * p:2 * p + 2, :].rearrange("p a b -> p (a b)"),
                                               start=True, stop=True)
                            mm.then_inc(sem(kind + "_in"), 1)

                        def attended_T(half, c):
                            kind = f"attT{half}"
                            pe.wait_ge(sem(f"o{2 * half + 1}_out"), c)
                            pe.wait_ge(sem(f"o{2 + half}_out"), c)
                            for j in range(4):
                                t = half * 4 + j
                                mm = pe.transpose(psum[BANK[kind]][:, j * P:(j + 1) * P],
                                                  att[:, 2 * t:2 * t + 2, :].rearrange("p a b -> p (a b)"), ident[:])
                            mm.then_inc(sem(kind + "_in"), 1)

                        def step(c, par):
                            nxt = 1 - par
                            front, back, tail = live(c, 1), live(c), live(c, -1)
                            last = live(c, -2)
                            if back:
                                features_T("tk0", c, par)
                                features_T("tq0", c, par)
                            if last:
                                pe.wait_ge(sem("hT_out"), times(c + 2, NCH))
                                pe.wait_ge(sem("h2_ready"), c - 1)
                                pe.transpose(psum[7][:, 0:P], h2_cur[par][:, 0:D], ident[:]).then_inc(sem("h2T_in"), 1)
                            if front:
                                pe.wait_ge(sem("h_split"), c + 2)
                                project("q0", c, nxt)
                                project("q1", c, nxt)
                            if last:
                                pe.wait_ge(sem("h2T_out"), c - 1)
                                pe.matmul(psum[7][:, 0:E], h2T[:], wg_sb[:], start=True, stop=True).then_inc(sem("lg_in"), 1)
                            if back:
                                features_T("tk1", c, par)
                                features_T("tq1", c, par)
                            if front:
                                project("k0", c, nxt)
                                project("k1", c, nxt)
                            if back:
                                score(0, c)
                            if tail:
                                attended_T(0, c)
                                attended_T(1, c)
                            if front:
                                project("pq0", c, nxt)
                                project("pq1", c, nxt)
                            if last:
                                pe.wait_ge(sem("lg_out"), c - 1)
                                pe.wait_ge(sem("hot_ready"), c - 1)
                                pe.matmul(psum[7][:, 0:2 * E], tri[:], hot[:], start=True, stop=True)
                                pe.matmul(psum[7][:, 2 * E:4 * E], ones[:], hot[:], start=True, stop=True).then_inc(sem("rank_in"), 1)
                            if back:
                                score(1, c)
                            if tail:
                                if last:
                                    pe.wait_ge(sem("rank_out"), c - 1)
                                else:
                                    pe.wait_ge(sem("hT_out"), times(c + 2, NCH))
                                pe.wait_ge(sem("attT0_out"), c)
                                pe.wait_ge(sem("attT1_out"), c)
                                for t in range(NP):
                                    mm = pe.matmul(psum[7][:, 0:D], attT[:, t, :], woT[:, t, :], start=(t == 0), stop=(t == NP - 1))
                                mm.then_inc(sem("wo_in"), 1)
                            if front:
                                project("pk0", c, nxt)
                                project("pk1", c, nxt)
                            if back:
                                pe.wait_ge(sem("v0_out"), c + 1)
                                pe.wait_ge(sem("v1_out"), c + 1)
                                state_gain(0, c, par)
                                attend(0, c, par)
                            if front:
                                project("v0", c, nxt)
                            if back:
                                attend(1, c, par)
                            if front:
                                project("v1", c, nxt)
                            if live(c, 2):
                                if tail:
                                    pe.wait_ge(sem("wo_out"), c)
                                else:
                                    pe.wait_ge(sem("hT_out"), times(c + 2))
                                pe.wait_ge(sem("xn_ready"), c + 3)
                                pe.transpose(psum[7][:, 0:P], xn[par][:], ident[:]).then_inc(sem("hT_in"), 1)
                            if back:
                                state_gain(1, c, par)
                                attend(2, c, par)
                                attend(3, c, par)
                                state_gain(2, c, par)
                        on_steps(pe, step)

                    @block.scalar
                    def _(act):
                        def step(c, par):
                            nxt = 1 - par
                            front, back, tail = live(c, 1), live(c), live(c, -1)

                            def features_T_out(half):
                                for k, bank in (("k", 2), ("q", 3)):
                                    act.wait_ge(sem(f"t{k}{half}_in"), c + 1)
                                    act.activation(phiT[k][:, half * 4:half * 4 + 4, :].rearrange("p a b -> p (a b)"),
                                                   psum[bank][:], ACT.Copy, scale=FEATURE_SCALE).then_inc(sem(f"t{k}{half}_out"), 1)

                            def squares(k):
                                act.wait_ge(sem(f"norm_{k}_ready"), c + 1)
                                for half in range(2):
                                    act.wait_ge(sem(f"{k}{half}_in"), c + 2)
                                    act.activation(square[k][:, half * 512:(half + 1) * 512], psum[half][:],
                                                   ACT.Square).then_inc(sem(f"{k}{half}_out"), 1)

                            def exps(k):
                                act.wait_ge(sem(f"p{k}0_out"), c + 2)
                                act.wait_ge(sem(f"p{k}1_out"), c + 2)
                                act.wait_ge(sem("tq1_in" if k == "q" else "kv2_in"), times(c))
                                act.activation(phi[k][nxt][:], expo[k][:], ACT.Exp).then_inc(sem(f"phi_{k}_ready"), 1)

                            last = live(c, -2)
                            if back:
                                features_T_out(0)
                            if last:
                                act.wait_ge(sem("h2T_in"), c - 1)
                                act.copy(h2T[:], psum[7][:, 0:P]).then_inc(sem("h2T_out"), 1)
                            if front:
                                squares("q")
                            if last:
                                act.wait_ge(sem("lg_in"), c - 1)
                                act.copy(lg_now[:], psum[7][:, 0:E]).then_inc(sem("lg_out"), 1)
                            if back:
                                features_T_out(1)
                            if front:
                                squares("k")
                            if last:
                                act.wait_ge(sem("choose_step"), 4 * (c - 1) - 1)
                                act.activation(prob[:], below[:], ACT.Exp).then_inc(sem("prob_ready"), 1)
                            if tail:
                                for half in range(2):
                                    act.wait_ge(sem(f"attT{half}_in"), c)
                                    act.copy(attT[:, half * 4:half * 4 + 4, :].rearrange("p a b -> p (a b)"),
                                             psum[4 + half][:]).then_inc(sem(f"attT{half}_out"), 1)
                            if front:
                                exps("q")
                                exps("k")
                                for half in range(2):
                                    act.wait_ge(sem(f"v{half}_in"), c + 2)
                                    act.wait_ge(sem("kv2_in"), times(c))
                                    act.copy(v_sb[nxt][:, half * 8:half * 8 + 8, 0:DH],
                                             psum[half][:].rearrange("p (h d) -> p h d", d=DH)).then_inc(sem(f"v{half}_out"), 1)
                            if live(c, 2):
                                act.wait_ge(sem("hT_in"), c + 3)
                                act.wait_ge(sem("h_split"), c + 2)
                                b = (c + 2) >> SHIFT
                                apart(act)
                                act.activation(h_full[:], psum[7][:, 0:P], ACT.Identity, bias=sa_col[:, bass.ds(b, 1)],
                                               scale=ca_col[:, bass.ds(b, 1)])
                                act.wait_ge(sem("v1_in"), times(c + 1))
                                apart(act)
                                act.activation(h_hi[par][:], psum[7][:, 0:P], ACT.Identity, bias=sa_col[:, bass.ds(b, 1)],
                                               scale=ca_col[:, bass.ds(b, 1)]).then_inc(sem("hT_out"), 1)
                        on_steps(act, step)

                    @block.vector
                    def _(dve):
                        def step(c, par):
                            nxt = 1 - par
                            front, back, tail = live(c, 1), live(c), live(c, -1)

                            def mask(g):
                                dve.wait_ge(sem(f"a{g}_in"), c + 1)
                                dve.tensor_tensor(scores[:, g * 4:g * 4 + 4, :], psum[BANK[f"a{g}"]][:].rearrange("p (h t) -> p h t", t=P),
                                                  causal[:], ALU.mult).then_inc(sem(f"a{g}_out"), 1)

                            def sum_squares(k):
                                dve.wait_ge(sem(f"{k}1_out"), c + 2)
                                dve.tensor_reduce(norm[k][:], square[k][:].rearrange("p (h d) -> p h d", d=DH), AX,
                                                  ALU.add).then_inc(sem(f"norm_{k}_ready"), 1)

                            def exponent(k):
                                dve.wait_ge(sem(f"norm_{k}_ready"), c + 2)
                                dve.wait_ge(sem(f"phi_{k}_ready"), c + 1)
                                for half in range(2):
                                    dve.wait_ge(sem(f"p{k}{half}_in"), c + 2)
                                    ins = dve.scalar_tensor_tensor(
                                        out=expo[k][:, half * 512:(half + 1) * 512].rearrange("p (h m) -> p h m", m=M),
                                        in0=norm[k][:, half * 8:half * 8 + 8].unsqueeze(2).to_broadcast([P, 8, M]), scalar=-0.5,
                                        in1=psum[half][:].rearrange("p (h m) -> p h m", m=M), op0=ALU.mult, op1=ALU.add)
                                    ins.then_inc(sem(f"p{k}{half}_out"), 1)

                            def normalise(g):
                                kind = f"o{g}"
                                o = psum[BANK[kind]][:, 0:2 * PW].rearrange("p (h w) -> p h w", w=VW)
                                dve.wait_ge(sem(kind + "_in"), c + 1)
                                dve.tensor_scalar(den[g % 2][:].unsqueeze(2), o[:, :, DH:VW], 1e-6, None, ALU.add).then_inc(sem("den_step"), 1)
                                dve.wait_ge(sem("den_step"), 8 * c + 2 * g + 1)
                                dve.reciprocal(rden[g % 2][:], den[g % 2][:]).then_inc(sem("den_step"), 1)
                                dve.wait_ge(sem("den_step"), 8 * c + 2 * g + 2)
                                dve.tensor_tensor(att[:, g * 4:g * 4 + 4, :], o[:, :, 0:DH],
                                                  rden[g % 2][:].unsqueeze(2).to_broadcast([P, 4, DH]), ALU.mult)\
                                   .then_inc(sem(kind + "_out"), 1)

                            def state_add(g):
                                kind = f"kv{g}"
                                dve.wait_ge(sem(kind + "_in"), c + 1)
                                n = len(KV_PAIRS[g])
                                p0 = KV_PAIRS[g][0]
                                gain = psum[6][:, 0:n * PW].rearrange("p (a w) -> p a w", w=PW)
                                for z in range(2):
                                    r, w = slice(z * M, (z + 1) * M), slice(z * VW, (z + 1) * VW)
                                    ins = dve.scalar_tensor_tensor(
                                        out=state[nxt][r, p0:p0 + n, w], in0=gain[r, :, w], scalar=FEATURE_SCALE,
                                        in1=state[par][r, p0:p0 + n, w], op0=ALU.mult, op1=ALU.add)
                                ins.then_inc(sem(kind + "_out"), 1)

                            def choose():
                                n = c - 1
                                dve.wait_ge(sem(f"sent{par}"), times(32 * ((c - 2) >> 1)))
                                dve.wait_ge(sem("lg_out"), n)
                                apart(dve)
                                dve.max(top[:], lg_now[:]).then_inc(sem("choose_step"), 1)
                                dve.wait_ge(sem("choose_step"), 4 * n - 3)
                                apart(dve)
                                dve.max_index(best[:], top[:], lg_now[:]).then_inc(sem("choose_step"), 1)
                                dve.tensor_scalar(below[:], top[:], top[:, 0:1], None, ALU.subtract).then_inc(sem("choose_step"), 1)
                                dve.wait_ge(sem("choose_step"), 4 * n - 2)
                                dve.tensor_copy(best_f[:], best[:, 0:2]).then_inc(sem("choose_step"), 1)
                                dve.wait_ge(sem("choose_step"), 4 * n)
                                dve.tensor_scalar(hot[:, 0:E], iota_e[:], best_f[:, 0:1], None, ALU.is_equal)
                                dve.tensor_scalar(hot[:, E:2 * E], iota_e[:], best_f[:, 1:2], -1.0, ALU.is_equal, ALU.mult)\
                                   .then_inc(sem("hot_ready"), 1)

                            def find_weights():
                                n = c - 1
                                dve.wait_ge(sem("prob_ready"), n)
                                dve.tensor_reduce(total[:], prob[:], AX, ALU.add).then_inc(sem("weight_step"), 1)
                                dve.wait_ge(sem("weight_step"), 6 * n - 5)
                                dve.reciprocal(total[:], total[:]).then_inc(sem("weight_step"), 1)
                                dve.wait_ge(sem("weight_step"), 6 * n - 4)
                                dve.tensor_scalar(pair[:], prob[:, 0:2], total[:, 0:1], None, ALU.mult).then_inc(sem("weight_step"), 1)
                                dve.wait_ge(sem("weight_step"), 6 * n - 3)
                                dve.tensor_reduce(total[:], pair[:], AX, ALU.add).then_inc(sem("weight_step"), 1)
                                dve.wait_ge(sem("weight_step"), 6 * n - 2)
                                dve.tensor_scalar(total[:], total[:], 1e-9, None, ALU.max).then_inc(sem("weight_step"), 1)
                                dve.wait_ge(sem("weight_step"), 6 * n - 1)
                                dve.reciprocal(total[:], total[:]).then_inc(sem("weight_step"), 1)
                                dve.wait_ge(sem("weight_step"), 6 * n)
                                dve.tensor_scalar(h2_cur[par][:, D + 1:D + 3], pair[:], total[:, 0:1], None, ALU.mult)

                            def find_places():
                                n = c - 1
                                dve.wait_ge(sem("rank_in"), n)
                                dve.tensor_tensor(place[:], psum[7][:, 0:2 * E], taken[:], ALU.add).then_inc(sem("slot_step"), 1)
                                dve.tensor_tensor(taken[:], psum[7][:, 2 * E:4 * E], taken[:], ALU.add).then_inc(sem("rank_out"), 1)

                            def find_slots():
                                n = c - 1
                                dve.wait_ge(sem("slot_step"), 5 * n - 4)
                                dve.tensor_tensor(over[:, 0:E], place[:, 0:E], first_limit[:], ALU.is_gt)
                                dve.tensor_tensor(over[:, E:2 * E], place[:, E:2 * E], second_limit[:], ALU.is_lt).then_inc(sem("slot_step"), 1)
                                dve.wait_ge(sem("slot_step"), 5 * n - 3)
                                dve.scalar_tensor_tensor(out=place[:], in0=over[:], scalar=float(SKIP), in1=place[:],
                                                         op0=ALU.mult, op1=ALU.add).then_inc(sem("slot_step"), 1)
                                dve.wait_ge(sem("slot_step"), 5 * n - 2)
                                dve.tensor_tensor(place[:], place[:], hot[:], ALU.mult).then_inc(sem("slot_step"), 1)
                                dve.wait_ge(sem("slot_step"), 5 * n - 1)
                                dve.tensor_reduce(slot_f[:], place[:].rearrange("p (k e) -> p k e", e=E), AX, ALU.add).then_inc(sem("slot_step"), 1)
                                dve.wait_ge(sem("slot_step"), 5 * n)
                                dve.tensor_tensor(slot[par][:], slot_f[:], sign[:], ALU.mult).then_inc(sem("slot_ready"), 1)

                            if back and par == 0:
                                dve.wait_ge(sem("kv2_out"), c)
                                st = state[par][:].bitcast(U32)
                                dve.tensor_scalar(st, st, keep[:, bass.ds(c, 1)], None, ALU.bitwise_and)\
                                   .then_inc(sem("state_kept"), 2)
                            if isinstance(c, int) and c == 0:
                                dve.wait_ge(sem("later_loads"), 16 * 6)
                            if front:
                                sum_squares("q")
                            if live(c, -2):
                                choose()
                                find_weights()
                            if back:
                                mask(0)
                                mask(1)
                            if live(c, 3):
                                first_moments(dve, c + 3)
                            if front:
                                exponent("q")
                            if live(c, -2):
                                find_places()
                            if front:
                                sum_squares("k")
                            if live(c, -2):
                                find_slots()
                            if back:
                                mask(2)
                                mask(3)
                            if tail:
                                dve.wait_ge(sem("x2_ready"), times(c - 1))
                                dve.wait_ge(sem("wo_in"), c)
                                dve.tensor_tensor(upd[0][:], psum[7][:, 0:D], bo_b[:], ALU.add).then_inc(sem("wo_out"), 1)
                            if front:
                                exponent("k")
                            if back:
                                state_add(0)
                            if tail:
                                dve.wait_ge(sem("x2_ready"), c)
                                moments(dve, "ln2", x2_now[:], st2, mv2, var2, c)
                            if back:
                                normalise(0)
                                normalise(1)
                            if back:
                                state_add(1)
                                normalise(2)
                            if live(c, 2):
                                dve.wait_ge(sem("hT_out"), c + 3)
                                dve.tensor_tensor(h_lo[par][:], h_full[:], h_hi[par][:].bitcast(F32), ALU.subtract).then_inc(sem("h_split"), 1)
                            if live(c, 3):
                                first_norm(dve, c + 3, nxt)
                            if back:
                                normalise(3)
                                state_add(2)
                        on_steps(dve, step)

                    @block.gpsimd
                    def _(pool):
                        def bound_gates():
                            for m, t in enumerate((ga_b, gb_b)):
                                g = t[:, 0:B * D]
                                pool.tensor_scalar(sgn[:], g, 0.0, 2.0, ALU.is_ge, ALU.mult).then_inc(sem("gate_step"), 1)
                                pool.wait_ge(sem("gate_step"), 5 * m + 1)
                                pool.tensor_scalar(sgn[:], sgn[:], -1.0, None, ALU.add).then_inc(sem("gate_step"), 1)
                                pool.wait_ge(sem("gate_step"), 5 * m + 2)
                                pool.tensor_tensor(mag[:], g, sgn[:], ALU.mult).then_inc(sem("gate_step"), 1)
                                pool.wait_ge(sem("gate_step"), 5 * m + 3)
                                pool.tensor_scalar(mag[:], mag[:], 0.25, None, ALU.max).then_inc(sem("gate_step"), 1)
                                pool.wait_ge(sem("gate_step"), 5 * m + 4)
                                pool.tensor_tensor(g, sgn[:], mag[:], ALU.mult).then_inc(sem("gate_step"), 1)
                                pool.wait_ge(sem("gate_step"), 5 * m + 5)

                        def step(c, par):
                            nxt = 1 - par
                            if live(c, -2):
                                pool.wait_ge(sem("slot_ready"), c - 1)
                                apart(pool)
                                for k in range(2):
                                    pool.indirect_dma_start(
                                        out=dispatched[:, :], in_=h2_cur[par][:], in_offset=None,
                                        out_offset=bass.IndirectOffsetOnAxis(ap=slot[par][:, k:k + 1].bitcast(U32), axis=0),
                                        bounds_check=2 * E * CAP - 1, oob_is_err=False).then_inc(sem(f"sent{par}"), 16)
                            if live(c, 3):
                                rstd(pool, "ln1", var1, rs1, c + 4)
                            if live(c, -1):
                                n = c - 1
                                b = n >> SHIFT
                                xs = x_sb[:, bass.ds(n * D, D)]
                                pool.wait_ge(sem("wo_out"), c)
                                apart(pool)
                                pool.tensor_tensor(upd[1][:], upd[0][:], ga_b[:, bass.ds(b * D, D)], ALU.mult).then_inc(sem("norm2_step"), 1)
                                pool.wait_ge(sem("norm2_step"), 3 * c - 2)
                                apart(pool)
                                pool.tensor_tensor(x2_now[:], xs, upd[1][:], ALU.add).then_inc(sem("x2_ready"), 1)
                                pool.wait_ge(sem("x2_ready"), c)
                                apart(pool)
                                pool.tensor_copy(xs, x2_now[:])
                                rstd(pool, "ln2", var2, rs2, c)
                                pool.wait_ge(sem("ln2_rstd"), c)
                                apart(pool)
                                pool.tensor_scalar(xn2[:], x2_now[:], mv2[:, 0:1], rs2[:, 0:1], ALU.subtract, ALU.mult).then_inc(sem("norm2_step"), 1)
                                pool.wait_ge(sem("norm2_step"), 3 * c - 1)
                                apart(pool)
                                pool.tensor_tensor(xm2[:], xn2[:], cb_b[:, bass.ds(b * D, D)], ALU.mult).then_inc(sem("norm2_step"), 1)
                                pool.wait_ge(sem("norm2_step"), 3 * c)
                                pool.wait_ge(sem(f"sent{nxt}"), times(32 * (n >> 1)))
                                pool.wait_ge(sem("h2T_in"), times(c - 2))
                                apart(pool)
                                pool.tensor_copy(h2_cur[nxt][:, D:D + 1], token[:, bass.ds(n, 1)])
                                pool.tensor_tensor(h2_cur[nxt][:, 0:D], xm2[:], sb_b[:, bass.ds(b * D, D)], ALU.add).then_inc(sem("h2_ready"), 1)
                            if isinstance(c, int) and c == -2:
                                for i in range(2):
                                    pool.memset(v_sb[i][:, :, DH:VW], 1.0)
                                    pool.memset(state[i][:], 0.0).then_inc(sem("state_zeroed"), 1)
                                pool.wait_ge(sem("state_zeroed"), 2)
                            if isinstance(c, int) and c == -1:
                                bound_gates()
                            if isinstance(c, int) and c == 1:
                                pool.wait_ge(sem("dispatched_blank"), 16 * (2 * E * CAP // (P * BLANK)))
                        on_steps(pool, step)
                        for par in range(2):
                            pool.wait_ge(sem(f"sent{par}"), 16 * NCH)

                    @block.sync
                    def _(sp):
                        for e in range(2):
                            sp.dma_start(w1_nat[e][:], w1_rows[e * P:(e + 1) * P, :]).then_inc(sem(f"w1_in{e}"), 16)
                            sp.dma_start(w2_sb[e][:], w2_rows[:, e * KH:(e + 1) * KH, :]).then_inc(sem(f"w2_in{e}"), 16)

        KV_PAIRS = [(0, 1, 2), (3, 4, 5), (6, 7)]
        h2_cur = [sb(f"h2_cur{i}", [P, RW]) for i in range(2)]
        attention()

        def experts():
            with ExitStack() as tmp:
                def tsb(name, shape, dt=F32):
                    return tmp.enter_context(nc.sbuf_tensor(name, shape, dt))
                GW = GS * P
                region = [[tsb(f"region{k}_{i}", [P, GS, RW]) for i in range(2)] for k in range(2)]
                rows = [tsb(f"rows{i}", [P, GS, RW]) for i in range(2)]
                rowsT_hi = [tsb(f"rowsT_hi{i}", [P, GW], F32R) for i in range(2)]
                rowsT_lo = [tsb(f"rowsT_lo{i}", [P, GW], F32R) for i in range(2)]
                hidden = [tsb(f"hidden{i}", [P, KH, GW]) for i in range(2)]
                y_sb = [tsb(f"y_sb{i}", [P, GS, D]) for i in range(2)]
                slot_id = [tsb(f"slot_id{i}", [P, GS], I32) for i in range(4)]
                row_id = [tsb(f"row_id{i}", [P, GS], I32) for i in range(2)]
                w1_hi = [tsb(f"w1_hi{i}", [P, HID], F32R) for i in range(2)]
                w1_lo = [tsb(f"w1_lo{i}", [P, HID], F32R) for i in range(2)]
                second = tsb("second", [P, NSL])
                slot_weight = [tsb(f"slot_weight{i}", [P, GS]) for i in range(4)]
                slot_rows = dispatched.rearrange("(a p) d -> p a d", p=P)
                GPE = TPE // GS
                BODY = 2 * GPE

                def on_groups(eng, step):
                    for j in range(BODY):
                        step(j, j, j // GPE)
                    with eng.Fori(1, NG // BODY - 1) as i:
                        for j in range(BODY):
                            step(i * BODY + j, j, i * 2 + j // GPE)
                    for j in range(BODY):
                        step(NG - BODY + j, j, E - 2 + j // GPE)

                def at_least(n, least):
                    return not isinstance(n, int) or n >= least

                def exists(e):
                    return not isinstance(e, int) or e < E

                with nc.Block() as block:
                    @block.sync
                    def _(sp):
                        def step(g, j, e):
                            par, w = j % 2, j // GPE
                            sp.wait_ge(sem("rows_ready"), times(g - 1))
                            for k in range(2):
                                sp.dma_start(region[k][par][:], slot_rows[:, bass.ds(g * GS + k * NSL, GS), :])\
                                  .then_inc(sem(f"region_in{par}"), 16)
                            if j % GPE == 0 and at_least(e, 1) and exists(e + 1):
                                sp.wait_ge(sem("w1_split"), e)
                                sp.dma_start(w1_nat[1 - w][:], w1_rows[bass.ds((e + 1) * P, P), :]).then_inc(sem(f"w1_in{1 - w}"), 16)
                        on_groups(sp, step)

                    @block.gpsimd
                    def _(pool):
                        def scatter(g, par):
                            pool.wait_ge(sem("y_out"), g + 1)
                            apart(pool)
                            for t in range(GS):
                                pool.indirect_dma_start(
                                    out=y_rows[:, :], out_offset=bass.IndirectOffsetOnAxis(ap=row_id[par][:, t:t + 1].bitcast(U32), axis=0),
                                    in_=y_sb[par][:, t, :], in_offset=None, bounds_check=2 * N - 1, oob_is_err=False,
                                ).then_inc(sem(f"y_stored{par}"), 16)
                        pool.wait_ge(sem("y_zeroed"), 16 * (2 * N // (P * BLANK)))
                        on_groups(pool, lambda g, j, e: scatter(g, j % 2))
                        for par in range(2):
                            pool.wait_ge(sem(f"y_stored{par}"), NG // 2 * 16 * GS)

                    @block.tensor
                    def _(pe):
                        def down(g, par, w):
                            pe.wait_ge(sem(f"w2_in{w}"), times(((g >> 2) + 1) * 16))
                            pe.wait_ge(sem("hid3_out"), g + 1)
                            pe.wait_ge(sem("y_out"), times(g - 1))
                            for t in range(GS):
                                for k in range(KH):
                                    mm = pe.matmul(psum[6 + par][:, t * D:(t + 1) * D], hidden[par][:, k, t * P:(t + 1) * P],
                                                   w2_sb[w][:, k, :], start=(k == 0), stop=(k == KH - 1))
                            mm.then_inc(sem("y_in"), 1)

                        def step(g, j, e):
                            par, w = j % 2, j // GPE
                            pe.wait_ge(sem("rows_ready"), g + 1)
                            pe.wait_ge(sem("rowsT_split"), times(g - 1))
                            for t in range(GS):
                                mm = pe.transpose(psum[par][:, t * P:(t + 1) * P], rows[par][:, t, 0:D], ident[:])
                            mm.then_inc(sem("rowsT_in"), 1)
                            if at_least(g, 2):
                                down(g - 2, par, 1 - w)
                            pe.wait_ge(sem("rowsT_split"), g + 1)
                            pe.wait_ge(sem("w1_split"), e + 1)
                            for k in range(KH):
                                pe.wait_ge(sem(f"hid{k}_out"), g)
                                o, ks = psum[2 + k][:], slice(k * P, (k + 1) * P)
                                pe.matmul(o, w1_hi[w][:, ks], rowsT_hi[par][:], start=True, stop=False)
                                pe.matmul(o, w1_lo[w][:, ks], rowsT_hi[par][:], start=False, stop=False)
                                pe.matmul(o, w1_hi[w][:, ks], rowsT_lo[par][:], start=False, stop=True).then_inc(sem(f"hid{k}_in"), 1)
                        on_groups(pe, step)
                        down(NG - 2, 0, 1)
                        down(NG - 1, 1, 1)

                    @block.scalar
                    def _(act):
                        def step(g, j, e):
                            par = j % 2
                            act.wait_ge(sem("rowsT_in"), g + 1)
                            act.wait_ge(sem("hid3_in"), times(g - 1))
                            act.copy(rowsT_hi[par][:], psum[par][:]).then_inc(sem("rowsT_hi_done"), 1)
                            act.wait_ge(sem("y_in"), times(g - 1))
                            for k in range(KH):
                                act.wait_ge(sem(f"hid{k}_in"), g + 1)
                                apart(act)
                                act.activation(hidden[par][:, k, :], psum[2 + k][:], ACT.Gelu,
                                               bias=b1_col[:, bass.ds(e * KH + k, 1)]).then_inc(sem(f"hid{k}_out"), 1)
                            if j % GPE == 1 and at_least(e, 1) and exists(e + 1):
                                w = j // GPE
                                act.wait_ge(sem("y_in"), g - 1)
                                act.dma_start(w2_sb[1 - w][:], w2_rows[:, bass.ds((e + 1) * KH, KH), :]).then_inc(sem(f"w2_in{1 - w}"), 16)
                        on_groups(act, step)

                    @block.vector
                    def _(dve):
                        def split_w1(e, w, g):
                            dve.wait_ge(sem(f"w1_in{w}"), ((e >> 1) + 1) * 16)
                            dve.wait_ge(sem("hid3_in"), times(g))
                            dve.tensor_copy(w1_hi[w][:], w1_nat[w][:]).then_inc(sem("w1_hi_done"), 1)
                            dve.wait_ge(sem("w1_hi_done"), e + 1)
                            dve.tensor_tensor(w1_lo[w][:], w1_nat[w][:], w1_hi[w][:].bitcast(F32), ALU.subtract).then_inc(sem("w1_split"), 1)

                        def merge(g, j, par):
                            dve.wait_ge(sem(f"region_in{par}"), ((g >> 1) + 1) * 32)
                            dve.wait_ge(sem("rowsT_in"), times(g - 1))
                            apart(dve)
                            dve.wait_ge(sem("y_out"), times(g - 3))
                            of = second[:, bass.ds(g * GS, GS)]
                            dve.tensor_tensor(slot_weight[j][:], region[1][par][:, :, D + 2], of, ALU.mult).then_inc(sem("merge_step"), 1)
                            dve.wait_ge(sem("merge_step"), g + 2)
                            dve.tensor_tensor(slot_weight[j][:], slot_weight[j][:], region[0][par][:, :, D + 1], ALU.add)
                            apart(dve)
                            for t in range(GS):
                                ins = dve.scalar_tensor_tensor(out=rows[par][:, t, :], in0=region[1][par][:, t, :],
                                                               scalar=second[:, bass.ds(g * GS + t, 1)],
                                                               in1=region[0][par][:, t, :], op0=ALU.mult, op1=ALU.add)
                            ins.then_inc(sem("rows_ready"), 1)
                            dve.wait_ge(sem("rows_ready"), g + 1)
                            apart(dve)
                            dve.scalar_tensor_tensor(out=slot_id[j][:], in0=second[:, bass.ds(g * GS, GS)], scalar=float(N),
                                                     in1=rows[par][:, :, D], op0=ALU.mult, op1=ALU.add).then_inc(sem("ids_ready"), 1)

                        def y_out(g, j, par, e):
                            dve.wait_ge(sem("y_in"), g + 1)
                            dve.wait_ge(sem(f"y_stored{par}"), times((g >> 1) * 16 * GS))
                            dve.tensor_copy(row_id[par][:], slot_id[j][:])
                            dve.tensor_tensor(y_sb[par][:], psum[6 + par][:].rearrange("p (t d) -> p t d", d=D),
                                              b2_b[:, bass.ds(e * D, D)].unsqueeze(1).to_broadcast([P, GS, D]), ALU.add)\
                               .then_inc(sem("y_sum"), 1)
                            dve.wait_ge(sem("y_sum"), g + 1)
                            dve.tensor_tensor(y_sb[par][:], y_sb[par][:], slot_weight[j][:].unsqueeze(2).to_broadcast([P, GS, D]), ALU.mult)\
                               .then_inc(sem("y_out"), 1)

                        dve.tensor_tensor(second[:].rearrange("p (e t) -> p e t", t=TPE),
                                          slot_number[:].rearrange("p (e t) -> p e t", t=TPE),
                                          taken[:, 0:E].unsqueeze(2).to_broadcast([P, E, TPE]), ALU.is_gt).then_inc(sem("merge_step"), 1)
                        dve.wait_ge(sem("merge_step"), 1)
                        def step(g, j, e):
                            par, w = j % 2, j // GPE
                            dve.wait_ge(sem("rowsT_hi_done"), g + 1)
                            dve.tensor_tensor(rowsT_lo[par][:], psum[par][:], rowsT_hi[par][:].bitcast(F32), ALU.subtract).then_inc(sem("rowsT_split"), 1)
                            if j % GPE == 1 and exists(e + 1):
                                split_w1(e + 1, 1 - w, g - 1)
                            if not isinstance(g, int) or g + 1 < NG:
                                merge(g + 1, (j + 1) % 4, 1 - par)
                            if at_least(g, 2):
                                y_out(g - 2, (j + 2) % 4, par, e - 1)
                        split_w1(0, 0, 0)
                        merge(0, 0, 0)
                        on_groups(dve, step)
                        y_out(NG - 2, 2, 0, E - 1)
                        y_out(NG - 1, 3, 1, E - 1)
        experts()

        def combine():
            with ExitStack() as tmp:
                def tsb(name, shape, dt=F32):
                    return tmp.enter_context(nc.sbuf_tensor(name, shape, dt))
                y = [[tsb(f"y{k}_{b}", [P, CPB, D]) for b in range(B)] for k in range(2)]
                y_v = y_rows.rearrange("(a p) d -> p a d", p=P)
                with nc.Block() as block:
                    @block.sync
                    def _(sp):
                        for b in range(B):
                            for k in range(2):
                                sp.dma_start(y[k][b][:], y_v[:, k * NCH + b * CPB:k * NCH + (b + 1) * CPB, :])\
                                  .then_inc(sem(f"y_loaded{b}"), 16)
                        for b in range(B):
                            if b < B - 1:
                                sp.wait_ge(sem("out_ready"), b + 1)
                            else:
                                sp.wait_ge(sem("combine_step"), 2 * B + 1)
                            sp.dma_start(out_v[:, b * CPB:(b + 1) * CPB, :],
                                         x_sb[:, b * CPB * D:(b + 1) * CPB * D].rearrange("p (c d) -> p c d", d=D)).then_inc(sem("out_stored"), 16)
                        sp.wait_ge(sem("out_stored"), 16 * B)

                    @block.vector
                    def _(dve):
                        for b in range(B):
                            y0, y1 = y[0][b][:], y[1][b][:]
                            dve.wait_ge(sem(f"y_loaded{b}"), 32)
                            dve.tensor_tensor(y0, y0, y1, ALU.add).then_inc(sem("combine_step"), 1)
                            dve.wait_ge(sem("combine_step"), 2 * b + 1)
                            dve.tensor_tensor(y0, y0, gb_b[:, b * D:(b + 1) * D].unsqueeze(1).to_broadcast([P, CPB, D]),
                                              ALU.mult).then_inc(sem("combine_step"), 1)
                        xs = x_sb[:, (B - 1) * CPB * D:B * CPB * D].rearrange("p (c d) -> p c d", d=D)
                        dve.wait_ge(sem("combine_step"), 2 * B)
                        dve.tensor_tensor(xs, xs, y[0][B - 1][:], ALU.add).then_inc(sem("combine_step"), 1)

                    @block.gpsimd
                    def _(pool):
                        for b in range(B - 1):
                            xs = x_sb[:, b * CPB * D:(b + 1) * CPB * D].rearrange("p (c d) -> p c d", d=D)
                            pool.wait_ge(sem("combine_step"), 2 * b + 2)
                            pool.tensor_tensor(xs, xs, y[0][b][:], ALU.add).then_inc(sem("out_ready"), 1)
        combine()


_INS = ["L0_attn_x", "L0_attn_omega", "L0_attn_wq", "L0_attn_wk", "L0_attn_wv", "L0_attn_wo", "L0_attn_bo",
        "L0_ffn_wg", "L0_ffn_w1", "L0_ffn_b1", "L0_ffn_w2", "L0_ffn_b2", "L0_c", "L0_wmod"]
_OUTS = [((4, 1024, 128), "float32")]


def kernel(**inputs):
    import numpy as _np
    import concourse.bacc as _bacc
    from concourse import mybir as _mybir
    from concourse.bass_utils import run_bass_kernel_spmd as _run

    nc = _bacc.Bacc("TRN2", target_bir_lowering=False, num_devices=1)
    arrays, args = {}, []
    for name in _INS:
        a = _np.ascontiguousarray(inputs[name])
        arrays[f"in_{name}_dram"] = a
        args.append(nc.dram_tensor(f"in_{name}_dram", a.shape, _mybir.dt.from_np(a.dtype), kind="ExternalInput").ap())
    for i, (shape, dtype) in enumerate(_OUTS):
        dt = _mybir.dt.from_np(_np.dtype(dtype))
        args.append(nc.dram_tensor(f"out_{i}_dram", shape, dt, kind="ExternalOutput").ap())
    build(nc, *args)
    r = _run(nc, [arrays], core_ids=[0])
    got = tuple(r.results[0][f"out_{i}_dram"] for i in range(len(_OUTS)))
    return got[0]
```
